# Optimizing a Trainium2 kernel written in Bass

```python
import numpy as np
import jax
import jax.numpy as jnp

def _softmax(x, axis=-1):
    return jax.nn.softmax(x, axis=axis)

def _gelu(x):
    return jax.nn.gelu(x, approximate=True)

def _silu(x):
    return jax.nn.silu(x)

def _sigmoid(x):
    return jax.nn.sigmoid(x)

def _layernorm(x, axis=-1, eps=1e-05):
    m = jnp.mean(x, axis=axis, keepdims=True)
    v = jnp.var(x, axis=axis, keepdims=True)
    return (x - m) / jnp.sqrt(v + eps)

def _scatter_add(tgt, idx, src, axis=0):
    return tgt.at[idx].add(src)

def _segment_sum(src, seg, n):
    return jax.ops.segment_sum(src, seg, n)
kernel_name = 'mk_xattn_ffn_d1_seqx_r8_baec4b'

def setup_inputs(seed: int=0):
    np.random.seed(seed)
    _w = jnp.asarray

    def _rec_inputs():
        import jax
        import jax.numpy as jnp
        _rk = jax.random.key(seed)
        x = -0.0002928 + 1 * jax.random.normal(jax.random.fold_in(_rk, 1), (4, 256, 128), jnp.float32)
        _lenS = 256 - jax.random.randint(jax.random.fold_in(_rk, 7), (4,), 0, max(1, 256 // 4) + 1, jnp.int32)
        _lenS2 = 1601 - jax.random.randint(jax.random.fold_in(_rk, 8), (4,), 0, max(1, 1601 // 4) + 1, jnp.int32)
        _ctx_1024P = jax.random.normal(jax.random.fold_in(_rk, 11), (4, 16, 128), jnp.float32)
        _ctx_1024c = jax.random.dirichlet(jax.random.fold_in(_rk, 511), 0.3 * jnp.ones((16,), jnp.float32), (4, 1601))
        _ctx_1024t = jnp.einsum('bsk,bkd->bsd', _ctx_1024c, _ctx_1024P)
        _ctx_1024t = _ctx_1024t * jax.lax.rsqrt(jnp.mean(jnp.square(_ctx_1024t)) + 1e-12) * 0.953939
        ctx_1024 = -1.39393e-06 + 0.999914 * (_ctx_1024t + 0.3 * jax.random.normal(jax.random.fold_in(_rk, 611), (4, 1601, 128), jnp.float32))
        return (x, ctx_1024)
    x, ctx_1024 = _rec_inputs()

    def _L0_xattn_setup():
        import math
        import jax, jax.numpy as jnp
        import numpy as np
        N_HEADS = 16
        TOPK_FACTOR = 0.5
        key = jax.random.key(seed)
        ks = jax.random.split(key, 11)
        B, L, D = (2, 256, 128)
        s = 0.02
        return {'q': jax.random.normal(ks[0], (B, L, D), jnp.float32), 'k': jax.random.normal(ks[1], (B, L, D), jnp.float32), 'v': jax.random.normal(ks[2], (B, L, D), jnp.float32), 'Wq': jax.random.normal(ks[3], (D, D), jnp.float32) * s, 'bq': jnp.zeros((D,), jnp.float32), 'Wk': jax.random.normal(ks[4], (D, D), jnp.float32) * s, 'bk': jnp.zeros((D,), jnp.float32), 'Wv': jax.random.normal(ks[5], (D, D), jnp.float32) * s, 'bv': jnp.zeros((D,), jnp.float32), 'Wo': jax.random.normal(ks[6], (D, D), jnp.float32) * s, 'bo': jnp.zeros((D,), jnp.float32)}
    _L0_xattn_all = _L0_xattn_setup()
    _L0_xattn_in = {k: v for k, v in _L0_xattn_all.items() if k in ('Wq', 'bq', 'Wk', 'bk', 'Wv', 'bv', 'Wo', 'bo')}
    del _L0_xattn_all

    def _L0_ffn_setup():
        import jax, jax.numpy as jnp
        import numpy as np
        LN_EPS = 1e-12
        key = jax.random.key(seed)
        ks = jax.random.split(key, 8)
        B, S, H, I, E = (4, 256, 128, 512, 8)
        sH = 1.0 / np.sqrt(H)
        sI = 1.0 / np.sqrt(I)
        return {'hidden_states': jax.random.normal(ks[0], (B, S, H), dtype=jnp.float32), 'Wr': jax.random.uniform(ks[1], (E, H), jnp.float32, -sH, sH), 'W1': jax.random.uniform(ks[2], (E, H, I), jnp.float32, -sH, sH), 'b1': jax.random.uniform(ks[3], (E, I), jnp.float32, -sH, sH), 'Wo': jax.random.uniform(ks[4], (I, H), jnp.float32, -sI, sI), 'bo': jax.random.uniform(ks[5], (H,), jnp.float32, -sI, sI), 'gamma': jnp.ones((H,), jnp.float32), 'beta': jnp.zeros((H,), jnp.float32)}
    _L0_ffn_all = _L0_ffn_setup()
    _L0_ffn_in = {k: v for k, v in _L0_ffn_all.items() if k in ('Wr', 'W1', 'b1', 'Wo', 'bo', 'gamma', 'beta')}
    del _L0_ffn_all
    return {'x': x, 'ctx_1024': ctx_1024, 'L0_xattn_Wq': _L0_xattn_in['Wq'], 'L0_xattn_bq': _L0_xattn_in['bq'], 'L0_xattn_Wk': _L0_xattn_in['Wk'], 'L0_xattn_bk': _L0_xattn_in['bk'], 'L0_xattn_Wv': _L0_xattn_in['Wv'], 'L0_xattn_bv': _L0_xattn_in['bv'], 'L0_xattn_Wo': _L0_xattn_in['Wo'], 'L0_xattn_bo': _L0_xattn_in['bo'], 'L0_ffn_Wr': _L0_ffn_in['Wr'], 'L0_ffn_W1': _L0_ffn_in['W1'], 'L0_ffn_b1': _L0_ffn_in['b1'], 'L0_ffn_Wo': _L0_ffn_in['Wo'], 'L0_ffn_bo': _L0_ffn_in['bo'], 'L0_ffn_gamma': _L0_ffn_in['gamma'], 'L0_ffn_beta': _L0_ffn_in['beta']}

def reference(x, ctx_1024, L0_xattn_Wq, L0_xattn_bq, L0_xattn_Wk, L0_xattn_bk, L0_xattn_Wv, L0_xattn_bv, L0_xattn_Wo, L0_xattn_bo, L0_ffn_Wr, L0_ffn_W1, L0_ffn_b1, L0_ffn_Wo, L0_ffn_bo, L0_ffn_gamma, L0_ffn_beta):
    import jax
    import jax.numpy as jnp

    def _L0_xattn_ref(q, k, v, Wq, bq, Wk, bk, Wv, bv, Wo, bo):
        import math
        import jax, jax.numpy as jnp
        import numpy as np
        N_HEADS = 16
        TOPK_FACTOR = 0.5
        B, Lq, D = q.shape
        Lk = k.shape[1]
        H = N_HEADS
        d_k = D // H
        Q = (q @ Wq.T + bq).reshape(B, Lq, H, d_k).transpose(0, 2, 1, 3)
        K = (k @ Wk.T + bk).reshape(B, Lk, H, d_k).transpose(0, 2, 1, 3)
        V = (v @ Wv.T + bv).reshape(B, Lk, H, d_k).transpose(0, 2, 1, 3)
        scores = jnp.einsum('bhqd,bhkd->bhqk', Q, K) / math.sqrt(d_k)
        topk = max(1, int(TOPK_FACTOR * Lk))
        topk_scores, topk_idx = jax.lax.top_k(scores, topk)
        sm = jax.nn.softmax(topk_scores, axis=-1)
        b_idx = jnp.arange(B)[:, None, None, None]
        h_idx = jnp.arange(H)[None, :, None, None]
        q_idx = jnp.arange(Lq)[None, None, :, None]
        attn = jnp.zeros_like(scores).at[b_idx, h_idx, q_idx, topk_idx].set(sm)
        ctx = jnp.einsum('bhqk,bhkd->bhqd', attn, V)
        ctx = ctx.transpose(0, 2, 1, 3).reshape(B, Lq, H * d_k)
        return ctx @ Wo.T + bo

    def _L0_ffn_ref(hidden_states, Wr, W1, b1, Wo, bo, gamma, beta):
        import jax, jax.numpy as jnp
        import numpy as np
        LN_EPS = 1e-12
        B, S, H = hidden_states.shape
        E = Wr.shape[0]
        x = hidden_states.reshape(-1, H)
        router_logits = x @ Wr.T
        expert_idx = jnp.argmax(jax.nn.softmax(router_logits, axis=-1), axis=-1)
        inter = jnp.zeros((x.shape[0], W1.shape[2]), dtype=x.dtype)
        for e in range(E):
            mask = (expert_idx == e)[:, None].astype(x.dtype)
            inter = inter + mask * jax.nn.gelu(x @ W1[e] + b1[e], approximate=False)
        y = inter @ Wo + bo + x
        mu = jnp.mean(y, axis=-1, keepdims=True)
        var = jnp.mean(jnp.square(y - mu), axis=-1, keepdims=True)
        out = (y - mu) * jax.lax.rsqrt(var + LN_EPS) * gamma + beta
        return out.reshape(B, S, H)
    x = x + _L0_xattn_ref(_layernorm(x, axis=-1), ctx_1024, ctx_1024, L0_xattn_Wq, L0_xattn_bq, L0_xattn_Wk, L0_xattn_bk, L0_xattn_Wv, L0_xattn_bv, L0_xattn_Wo, L0_xattn_bo)
    x = x + _L0_ffn_ref(_layernorm(x, axis=-1), L0_ffn_Wr, L0_ffn_W1, L0_ffn_b1, L0_ffn_Wo, L0_ffn_bo, L0_ffn_gamma, L0_ffn_beta)
    return x

_drawn_inputs = setup_inputs


def setup_inputs(seed=0):
    import zlib

    import numpy as np

    out = dict(_drawn_inputs(seed))
    spreads = {'L0_xattn_bq': (0.0, 2.0),
     'L0_xattn_bk': (0.0, 2.0),
     'L0_xattn_bv': (0.0, 0.1),
     'L0_xattn_bo': (0.0, 0.1),
     'L0_ffn_gamma': (1.0, 0.2),
     'L0_ffn_beta': (0.0, 0.1)}
    factors = {'L0_xattn_Wq': 5.948, 'L0_xattn_Wk': 5.331, 'L0_ffn_b1': 6.172, 'L0_ffn_bo': 3.989}
    for name, (base, spread) in spreads.items():
        noise = np.random.default_rng([zlib.crc32(name.encode()), seed]).standard_normal(out[name].shape)
        drawn = base * np.exp(spread * noise) if base else spread * noise
        out[name] = jnp.asarray(drawn.astype(out[name].dtype))
    for name, factor in factors.items():
        out[name] = (out[name] * factor).astype(out[name].dtype)
    return out
```

```python
from contextlib import ExitStack

import numpy as np
import concourse.bass as bass
from concourse import mybir

F32 = mybir.dt.float32
BF16 = mybir.dt.bfloat16
I32 = mybir.dt.int32
ALU = mybir.AluOpType
ACT = mybir.ActivationFunctionType
AX = mybir.AxisListType

P = 128
B, L, D = 4, 256, 128
NK = 1601
H, DH = 16, 8
TOPK = NK // 2
NI, NE = 512, 8
KC = 13
KR = NK - (KC - 1) * P
QT = L // P
G = 2 * QT
NG = B * H * QT // G
NT = B * H * QT
RING = 4
CUT = 1024
PART = DH * 3

NSEG = 8
SEG = NK // NSEG
NV = 24
AIM = 8
LAST_AIM = 9
LEAN = 0.2
SHIFT = 1.0
SLOPE = 1.0 / (2 * NK * 0.4)
STIFF = 600.0
BISECT = 48
BIG = 1e30
LOST = 1024.0
MOST = P * (int(LOST) + 1)
QSCALE = float(1.0 / np.sqrt(DH))


def build(nc, x, ctx, ctxT, WqT, bq, WkT, bk, WvT, bv, WoT, bo, WrT, W1, b1, Wf, bf, gamma, beta,
          ident_in, blocks_in, heads_in, ranks_in, firsts_in, out):
    with ExitStack() as es:
        def sb(name, shape, dt=F32):
            return es.enter_context(nc.sbuf_tensor(name, shape, dt))

        def sem(name):
            return es.enter_context(nc.semaphore(name))

        k_parts = nc.dram_tensor("k_parts", [B * H * PART, NK], BF16).ap()
        q_parts = [nc.dram_tensor(f"q_parts{g}", [B * H * PART, L], BF16).ap() for g in range(3)]
        heads_T = nc.dram_tensor("heads_T", [B * H * DH, L], F32).ap()

        S = sb("S", [P, RING * G * NK])
        y = sb("y", [P, NK])
        E = [sb(f"E{i}", [P, NK]) for i in range(2)]
        signs = sb("signs", [P, G, NK], mybir.dt.int8)
        kst = sb("kst", [P, 4, NK], BF16)
        qst = sb("qst", [P, 4, L], BF16)
        PT = [sb(f"PT{i}", [P, KC, L]) for i in range(2)]
        V_all = sb("V_all", [P, KC, B * D])
        vst = [sb(f"vst{i}", [P, KC, DH]) for i in range(2)]
        osb = [sb(f"osb{i}", [DH, L]) for i in range(2)]
        cand = sb("cand", [P, G, NSEG * 8])
        cand2 = sb("cand2", [P, G, NSEG * 8])
        top = sb("top", [P, G, NV])
        hit = sb("hit", [P, G, NV - 1])
        pick = sb("pick", [P, G, NV - 1])
        trial = sb("trial", [P, G])
        rank = sb("rank", [P, G])
        nxt = sb("nxt", [P, G])
        seg8 = sb("seg8", [P, G])
        bad = sb("bad", [P, G])
        bad2 = sb("bad2", [P, G])
        badf = sb("badf", [1, 1])
        badi = sb("badi", [1, G + 1], I32)
        mx = sb("mx", [P, G, 2])
        shift = sb("shift", [P, NT])
        unit = sb("unit", [P, NT])
        nthr = sb("nthr", [P, NT])
        thr = sb("thr", [P, NT])
        nmax = sb("nmax", [P, NT])
        sgn = sb("sgn", [P, NT])
        fprev = sb("fprev", [P, NT])
        step_c = sb("step_c", [P, NT])
        ratio = sb("ratio", [P, NT])
        Z = sb("Z", [P, NT])
        c_aim = sb("c_aim", [P, G // 2])
        c_one = sb("c_one", [P, G // 2])
        c_stiff = sb("c_stiff", [P, G // 2])
        c_neg = sb("c_neg", [P, G // 2])
        g_wait, a_wait = sb("g_wait", [P, G // 2]), sb("a_wait", [P, 2])
        g_f = sb("g_f", [P, G // 2])
        g_df = sb("g_df", [P, G // 2])
        g_num = sb("g_num", [P, G // 2])
        g_old = sb("g_old", [P, G // 2])
        g_den = sb("g_den", [P, G // 2])
        g_r = sb("g_r", [P, G // 2])
        g_e = sb("g_e", [P, G // 2])
        g_d = sb("g_d", [P, G // 2])
        lo, hi, mid, cnt, keep, w0, w1, w2 = (sb(n, [P, 1]) for n in ("lo", "hi", "mid", "cnt", "keep", "w0", "w1", "w2"))
        ident = sb("ident", [P, P])
        heads1 = sb("heads1", [P, H])
        ranks = sb("ranks", [P, NV - 1])
        firsts = sb("firsts", [P, NE])
        ones = sb("ones", [P, 1])
        wo = sb("wo", [P, D])
        wr = sb("wr", [P, NE])
        bqc, bkc = sb("bqc", [P, 1]), sb("bkc", [P, 1])
        bob, bfb, gab, beb = (sb(n, [P, D]) for n in ("bob", "bfb", "gab", "beb"))
        eps5, eps12 = sb("eps5", [P, 1]), sb("eps12", [P, 1])

        ps = es.enter_context(nc.psum_tensor("ps", [P, 8, 512], F32))
        psf = ps[:].rearrange("p a b -> p (a b)")

        used = [0]

        def carve(n, dt=F32):
            a = S[:, used[0]:used[0] + n]
            used[0] += n
            if dt == BF16:
                a = a.bitcast(BF16)
            return a

        wq, wk, wv, bvb, blocks = (carve(D) for _ in range(5))
        cT = carve(NK)
        cx = carve(KC * (D + 1)).rearrange("p (c d) -> p c d", c=KC)
        kf = carve(NK)
        kres = carve(NK)
        kp = [carve(NK // 2 + 1, BF16)[:, 0:NK] for _ in range(3)]
        xin = carve(QT * D).rearrange("p (t d) -> p t d", t=QT)
        xn = carve(QT * D).rearrange("p (t d) -> p t d", t=QT)
        xnT = carve(L)
        qf = carve(L)
        qres = carve(L)
        qp = [carve(L // 2, BF16) for _ in range(3)]
        gram = carve(D + 1)
        t1 = carve(D)
        krow = carve(D)
        nkrow = carve(D)
        cov = carve(D)
        mb = carve(H)
        kb = carve(1)
        zq = carve(L)
        var = carve(QT * H).rearrange("p (t h) -> p t h", t=QT)
        sig = carve(QT * H).rearrange("p (t h) -> p t h", t=QT)
        stats = carve(QT * 6).rearrange("p (t s) -> p t s", t=QT)
        agg = carve(QT * 2).rearrange("p (t s) -> p t s", t=QT)
        rstd = carve(QT)
        assert used[0] <= RING * G * NK
        used[0] = 0
        w1s = carve(NE * NI).rearrange("p (e n) -> p e n", e=NE)
        wfs = carve(NI // P * D).rearrange("p (c d) -> p c d", c=NI // P)
        b1s = carve(NI)
        ecT = carve(P)
        ex = carve(D)
        ecn = carve(D)
        ecnT = carve(P)
        ex1 = carve(D)
        exn = carve(D)
        exnT = carve(P)
        elog = carve(NE)
        emx = carve(1)
        eone = carve(NE)
        eoneT = carve(P)
        eacc = carve(NI)
        egel = carve(NI)
        egT = carve(NI)
        ey = carve(D)
        erz = carve(H)
        est = carve(6)
        eag = carve(2)
        ers = carve(1)
        eout = carve(D)

        s_const = sem("s_const")
        s_cset = sem("s_cset")
        s_pin = sem("s_pin")
        s_ppe = sem("s_ppe")
        s_pdve = sem("s_pdve")
        s_pst = sem("s_pst")
        s_pact = sem("s_pact")
        s_pout = sem("s_pout")
        s_stk = sem("s_stk")
        s_sc = sem("s_sc")
        s_ev = sem("s_ev")
        s_nm = sem("s_nm")
        s_cnt = [sem(f"s_cnt{i}") for i in range(4)]
        s_thr = [sem(f"s_thr{i}") for i in range(4)]
        s_badr = sem("s_badr")
        s_badc = sem("s_badc")
        s_sel = sem("s_sel")
        s_exp = sem("s_exp")
        s_p = sem("s_p")
        s_ta = sem("s_ta")
        s_tb = sem("s_tb")
        s_ca = sem("s_ca")
        s_cb = sem("s_cb")
        s_vst = sem("s_vst")
        s_av = sem("s_av")
        s_ao = sem("s_ao")
        s_aw = [sem(f"s_aw{a}") for a in range(2)]
        s_ein = sem("s_ein")
        s_ew = sem("s_ew")
        s_epe = sem("s_epe")
        s_edve = sem("s_edve")
        s_eact = sem("s_eact")
        s_out = sem("s_out")

        NCONST = 17
        NPE, NDV, NAC = 9, 10, 4
        EPE, EDV, EAC = 14, 19, 8

        def S_at(slot, k, a=0, n=NK):
            return S[:, bass.ds((slot * G + k) * NK + a, n)]

        def col(t, n=1):
            return bass.ds(t, n)

        def steps(eng, run):
            def stages(s):
                return [0 <= s - i < NG for i in range(5)] + [s + 1 < NG]
            for s in range(4):
                run(s, stages(s))
            with eng.Fori(4, NG - 1) as s:
                run(s, [True] * 6)
            for s in range(NG - 1, NG + 4):
                run(s, stages(s))

        block = es.enter_context(nc.Block())

        @block.sync
        def _(sp):
            consts = [(ident, ident_in), (blocks, blocks_in), (heads1, heads_in), (ranks, ranks_in), (firsts, firsts_in),
                      (wq, WqT), (wk, WkT), (wv, WvT), (wo, WoT), (wr, WrT),
                      (bqc, bq.rearrange("(p a) -> p a", a=1)), (bkc, bk.rearrange("(p a) -> p a", a=1))]
            for dst, src in consts:
                sp.dma_start(dst[:, :], src).then_inc(s_const, 16)
            for dst, src in ((bvb, bv), (bob, bo), (bfb, bf), (gab, gamma), (beb, beta)):
                sp.dma_start(dst[:, :], src.rearrange("(a d) -> a d", a=1).broadcast_to([P, D])).then_inc(s_const, 16)
            sp.wait_ge(s_cset, 1)
            full = (KC - 1) * P
            with sp.Fori(0, B) as b:
                sp.wait_ge(s_pdve, b * NDV)
                sp.dma_start(cT, ctxT[bass.ds(b * D, D), :]).then_inc(s_pin, 16)
                sp.dma_start(cx[:, 0:KC - 1, 0:D],
                             ctx[bass.ds(b * NK, full), :].rearrange("(c p) d -> p c d", p=P)).then_inc(s_pin, 16)
                sp.dma_start(cx[0:KR, KC - 1, 0:D], ctx[bass.ds(b * NK + full, KR), :]).then_inc(s_pin, 16)
                sp.dma_start(xin, x[bass.ds(b * L, L), :].rearrange("(t p) d -> p t d", p=P)).then_inc(s_pin, 16)
                sp.wait_ge(s_pdve, b * NDV + 5)
                for g in range(3):
                    dst = q_parts[g][bass.ds(b * H * PART, H * PART), :].rearrange("(r j) q -> r j q", j=3)
                    for j in range(3):
                        sp.dma_start(dst[:, j, :], qp[g]).then_inc(s_pout, 16)
                sp.wait_ge(s_pdve, b * NDV + 10)
                dst = k_parts[bass.ds(b * H * PART, H * PART), :].rearrange("(r j) k -> r j k", j=3)
                for j in range(3):
                    sp.dma_start(dst[:, j, :], kp[j]).then_inc(s_pout, 16)
            sp.wait_ge(s_pout, B * 12 * 16)

            def stacked(s):
                if not isinstance(s, int) or s >= 2:
                    sp.wait_ge(s_sc, 2 * G * (s - 1))
                if not isinstance(s, int) or s >= 1:
                    sp.wait_ge(s_stk, 96 * s)
                slot = s % 2 * 2
                for g in range(3):
                    sp.dma_start(kst[32 * g:32 * g + PART, bass.ds(slot, 2), :],
                                 k_parts[bass.ds(s * 2 * PART, 2 * PART), :]
                                 .rearrange("(a r) k -> r a k", a=2)).then_inc(s_stk, 16)
                    sp.dma_start(qst[32 * g:32 * g + PART, bass.ds(slot, 2), :],
                                 q_parts[g][bass.ds(s * 2 * PART, 2 * PART), :]
                                 .rearrange("(a r) k -> r a k", a=2)).then_inc(s_stk, 16)

            stacked(0)

            def run(s, on):
                if on[5]:
                    stacked(s + 1)
                if on[4]:
                    sp.wait_ge(s_ao, 2 * (s - 4) + 2)
                    sp.dma_start(heads_T[bass.ds((s - 4) * 2 * DH + DH, DH), :], osb[1][:]).then_inc(s_aw[1], 16)
                if on[3]:
                    sp.wait_ge(s_ao, 2 * (s - 3) + 1)
                    sp.dma_start(heads_T[bass.ds((s - 3) * 2 * DH, DH), :], osb[0][:]).then_inc(s_aw[0], 16)
            steps(sp, run)

            sp.wait_ge(s_p, NT)
            sp.wait_ge(s_exp, NT)
            sp.dma_start(w1s, W1.rearrange("e d n -> d e n")).then_inc(s_ew, 16)
            sp.dma_start(wfs, Wf.rearrange("(c p) d -> p c d", p=P)).then_inc(s_ew, 16)
            sp.dma_start(b1s[0:NE, :], b1).then_inc(s_ew, 16)
            sp.wait_ge(s_aw[0], 16 * NG)
            sp.wait_ge(s_aw[1], 16 * NG)
            with sp.Fori(0, B * QT) as n:
                sp.wait_ge(s_edve, n * EDV)
                sp.dma_start(ecT, heads_T[bass.ds(n // QT * D, D), bass.ds(n % QT * P, P)]).then_inc(s_ein, 16)
                sp.dma_start(ex, x[bass.ds(n * P, P), :]).then_inc(s_ein, 16)
                sp.wait_ge(s_edve, n * EDV + EDV)
                sp.dma_start(out[bass.ds(n * P, P), :], eout).then_inc(s_out, 16)
            sp.wait_ge(s_out, 16 * B * QT)

        @block.gpsimd
        def _(pool):
            pool.memset(kst[:], 0.0)
            pool.memset(qst[:], 0.0)
            pool.memset(ones[:], 1.0)
            pool.memset(eps5[:], 1e-5)
            pool.memset(eps12[:], 1e-12)
            pool.memset(cx[:, :, D:D + 1], 1.0)
            pool.memset(c_aim[:], float(NK - 2 * (TOPK - AIM)))
            pool.memset(c_one[:], 1.0)
            pool.memset(c_stiff[:], STIFF)
            pool.memset(c_neg[:], -1.0)
            pool.memset(ratio[:], 1.0)
            pool.drain().then_inc(s_cset, 1)

            def correct(g, r, h):
                c = col(g * G + h * G // 2, G // 2)
                pool.wait_ge(s_cnt[r], G * g + (h + 1) * G // 2)
                pool.tensor_tensor(g_wait[:], c_one[:], c_one[:], ALU.mult)
                pool.tensor_tensor(g_f[:], sgn[:, c], c_aim[:], ALU.add)
                pool.drain()
                if r > 0:
                    pool.tensor_tensor(g_df[:], fprev[:, c], g_f[:], ALU.subtract)
                    pool.tensor_tensor(g_old[:], ratio[:, c], c_stiff[:], ALU.mult)
                    pool.drain()
                    pool.tensor_tensor(g_num[:], step_c[:, c], g_df[:], ALU.mult)
                    pool.tensor_tensor(g_den[:], g_df[:], g_df[:], ALU.mult)
                    pool.drain()
                    pool.tensor_tensor(g_num[:], g_num[:], g_old[:], ALU.add)
                    pool.tensor_tensor(g_den[:], g_den[:], c_stiff[:], ALU.add)
                    pool.drain()
                    pool.tensor_tensor(g_den[:], g_den[:], c_neg[:], ALU.pow)
                    pool.drain()
                    pool.tensor_tensor(g_r[:], g_num[:], g_den[:], ALU.mult)
                    pool.drain()
                    pool.tensor_scalar(g_r[:], g_r[:], 0.4, 2.2, ALU.max, ALU.min)
                    pool.drain()
                    pool.tensor_tensor(g_d[:], g_f[:], g_r[:], ALU.mult)
                else:
                    pool.tensor_tensor(g_d[:], g_f[:], c_one[:], ALU.mult)
                if r < 2:
                    pool.tensor_tensor(fprev[:, c], g_f[:], c_one[:], ALU.mult)
                    if r > 0:
                        pool.tensor_tensor(ratio[:, c], g_r[:], c_one[:], ALU.mult)
                    pool.drain()
                    pool.tensor_tensor(step_c[:, c], g_d[:], c_one[:], ALU.mult)
                else:
                    pool.drain()
                    pool.tensor_scalar(g_num[:], g_d[:], 0.0, 2 * LEAN, ALU.max, ALU.mult)
                    pool.tensor_scalar(g_den[:], g_d[:], 1 - LEAN, 2.0 * (LAST_AIM - AIM), ALU.mult, ALU.add)
                    pool.drain()
                    pool.tensor_tensor(g_d[:], g_num[:], g_den[:], ALU.add)
                    pool.drain()
                pool.tensor_tensor(g_e[:], g_d[:], unit[:, c], ALU.mult)
                pool.drain()
                pool.tensor_tensor(nthr[:, c], nthr[:, c], g_e[:], ALU.subtract).then_inc(s_thr[r + 1], 1)

            def lay_v(g, a):
                if not isinstance(g, int) or g >= 1:
                    pool.wait_ge(s_av, 2 * g - 1 + a)
                pool.tensor_copy(vst[a][:, 0:KC - 1, :],
                                 V_all[:, 0:KC - 1, bass.ds(g * 2 * DH + a * DH, DH)])
                pool.tensor_copy(vst[a][0:KR, KC - 1, :],
                                 V_all[0:KR, KC - 1, bass.ds(g * 2 * DH + a * DH, DH)]).then_inc(s_vst, 1)

            pool.wait_ge(s_pdve, B * NDV)

            def run(s, on):
                if on[1]:
                    for h in range(2):
                        correct(s - 1, 0, h)
                if on[3]:
                    lay_v(s - 3, 0)
                if on[1]:
                    for r in range(1, 3):
                        for h in range(2):
                            correct(s - 1, r, h)
                if on[3]:
                    lay_v(s - 3, 1)
            steps(pool, run)

        @block.scalar
        def _(act):
            with act.Fori(0, B) as b:
                act.wait_ge(s_pst, b + 1)
                act.activation(rstd, agg[:, :, 1], ACT.Sqrt, bias=eps5[:]).then_inc(s_pact, 1)
                act.wait_ge(s_pdve, b * NDV)
                act.wait_ge(s_ppe, b * NPE + 2)
                act.activation(kf, psf[:, 0:NK], ACT.Identity, bias=bkc[:]).then_inc(s_pact, 1)
                act.wait_ge(s_ppe, b * NPE + 4)
                act.activation(xnT, ps[:, 4, 0:L], ACT.Copy).then_inc(s_pact, 1)
                act.wait_ge(s_pdve, b * NDV + 8)
                act.activation(sig, var, ACT.Sqrt).then_inc(s_pact, 1)
            act.wait_ge(s_pdve, B * NDV)

            def count(g, r, k):
                t = g * G + k
                if r == 0:
                    if k == 0 and (not isinstance(g, int) or g >= 1):
                        act.wait_ge(s_cnt[3], G * g)
                    act.wait_ge(s_ev, 2 * G * g + 2 * k + 2)
                elif k % 2 == 0:
                    act.wait_ge(s_thr[r], 2 * g + k // 2 + 1)
                    act.activation(a_wait[:, k // 2:k // 2 + 1], ones[:], ACT.Copy)
                act.activation(signs[:, k, :], S_at(g % RING, k), ACT.Sign, bias=nthr[:, col(t)],
                               accum_out=sgn[:, col(t)]).then_inc(s_cnt[r], 1)

            def copy_a(g, k):
                act.wait_ge(s_ta, g * G + k + 1)
                if k % 2 == 0 and (not isinstance(g, int) or g >= 1):
                    act.wait_ge(s_av, 2 * g - 1 + k // 2)
                for i in range(2):
                    ins = act.activation(PT[k // 2][:, 4 * i:4 * i + 4, k % 2 * P:k % 2 * P + P],
                                         ps[:, 4 + i, :].rearrange("p (c q) -> p c q", c=4), ACT.Copy)
                ins.then_inc(s_ca, 1)

            def copy_b(g, k):
                act.wait_ge(s_tb, g * G + k + 1)
                q = slice(k % 2 * P, k % 2 * P + P)
                act.activation(PT[k // 2][:, 8:12, q], ps[:, 4, :].rearrange("p (c q) -> p c q", c=4), ACT.Copy)
                act.activation(PT[k // 2][0:KR, 12, q], ps[0:KR, 5, 0:P], ACT.Copy).then_inc(s_cb, 1)

            def head_out(g, a):
                act.wait_ge(s_av, 2 * g + a + 1)
                if not isinstance(g, int) or g >= 1:
                    act.wait_ge(s_aw[a], 16 * g)
                act.activation(osb[a][:], ps[0:DH, 6, 0:L], ACT.Copy).then_inc(s_ao, 1)

            def run(s, on):
                for k in range(G):
                    if on[1]:
                        count(s - 1, k, 0)
                        count(s - 1, k, 1)
                    if on[3]:
                        t = (s - 3) * G + k
                        if k == 0:
                            act.wait_ge(s_sel, s - 2)
                        if k >= 2 or not isinstance(s, int) or s > 3:
                            act.wait_ge(s_tb, t - 1)
                        act.activation(E[k % 2][:], S_at((s - 3) % RING, k), ACT.Exp,
                                       bias=nmax[:, col(t)]).then_inc(s_exp, 1)
                    if k > 0 and on[3]:
                        copy_a(s - 3, k - 1)
                    if k == 0 and on[4]:
                        copy_a(s - 4, G - 1)
                    if k == 2 and on[4]:
                        head_out(s - 4, 1)
                    if on[1]:
                        count(s - 1, k, 2)
                    if k == 0 and on[4]:
                        copy_b(s - 4, G - 1)
                    if k > 0 and on[3]:
                        copy_b(s - 3, k - 1)
                    if on[1]:
                        count(s - 1, k, 3)
                    if k == 3 and on[3]:
                        head_out(s - 3, 0)
            steps(act, run)

            with act.Fori(0, B * QT) as n:
                act.wait_ge(s_epe, n * EPE + 2)
                act.activation(ecnT, ps[:, 1, 0:P], ACT.Copy).then_inc(s_eact, 1)
                act.wait_ge(s_edve, n * EDV + 4)
                act.activation(ers, eag[:, 1:2], ACT.Sqrt, bias=eps5[:]).then_inc(s_eact, 1)
                act.wait_ge(s_epe, n * EPE + 4)
                act.activation(exnT, ps[:, 3, 0:P], ACT.Copy).then_inc(s_eact, 1)
                act.wait_ge(s_epe, n * EPE + 6)
                act.activation(eoneT[0:NE, :], ps[0:NE, 1, 0:P], ACT.Copy).then_inc(s_eact, 1)
                act.wait_ge(s_epe, n * EPE + 7)
                act.activation(eacc, ps[:, 2, :], ACT.Copy).then_inc(s_eact, 1)
                act.wait_ge(s_edve, n * EDV + 16)
                act.activation(egel, eacc, ACT.Gelu).then_inc(s_eact, 1)
                act.wait_ge(s_epe, n * EPE + 12)
                act.activation(egT, ps[:, 1, :], ACT.Copy).then_inc(s_eact, 1)
                act.wait_ge(s_edve, n * EDV + 18)
                act.activation(ers, eag[:, 1:2], ACT.Sqrt, bias=eps12[:]).then_inc(s_eact, 1)

        @block.tensor
        def _(pe):
            pe.wait_ge(s_const, 16 * NCONST)
            pe.wait_ge(s_cset, 1)
            with pe.Fori(0, B) as b:
                last = b * NPE
                pe.wait_ge(s_pin, 64 * (b + 1))
                pe.wait_ge(s_pdve, b * NDV)
                vps = psf[:, 4 * 512:4 * 512 + KC * P].rearrange("p (c d) -> p c d", c=KC)
                for c in range(KC):
                    m = P if c < KC - 1 else KR
                    mm = pe.matmul(vps[0:m, c, :], cT[:, c * P:c * P + m], wv, start=True, stop=True)
                mm.then_inc(s_ppe, 1)
                for c in range(4):
                    n = min(512, NK - 512 * c)
                    mm = pe.matmul(ps[:, c, 0:n], wk, cT[:, 512 * c:512 * c + n], start=True, stop=True)
                mm.then_inc(s_ppe, 1)
                pe.wait_ge(s_pdve, b * NDV + 2)
                for c in range(KC):
                    m = P if c < KC - 1 else KR
                    mm = pe.matmul(ps[:, 6, 0:D + 1], cx[0:m, c, 0:D], cx[0:m, c, :],
                                   start=(c == 0), stop=(c == KC - 1))
                mm.then_inc(s_ppe, 1)
                for t in range(QT):
                    mm = pe.transpose(ps[:, 4, t * P:t * P + P], xn[:, t, :], ident[:])
                mm.then_inc(s_ppe, 1)
                pe.wait_ge(s_pdve, b * NDV + 3)
                pe.matmul(ps[:, 7, 0:D], gram[:, 0:D], wk, start=True, stop=True)
                pe.matmul(ps[0:1, 7, D:2 * D], gram[:, D:D + 1], wk, start=True, stop=True)
                pe.matmul(ps[:, 7, 2 * D:2 * D + 1], wk, gram[:, D:D + 1],
                          start=True, stop=True).then_inc(s_ppe, 1)
                pe.wait_ge(s_pact, b * NAC + 3)
                pe.matmul(ps[:, 5, 0:L], wq, xnT, start=True, stop=True).then_inc(s_ppe, 1)
                pe.wait_ge(s_pdve, b * NDV + 4)
                pe.matmul(ps[:, 6, 0:D], wk, t1, start=True, stop=False)
                pe.matmul(ps[:, 6, 0:D], krow[0:1, :], nkrow[0:1, :],
                          start=False, stop=True).then_inc(s_ppe, 1)
                pe.wait_ge(s_pdve, b * NDV + 6)
                pe.matmul(ps[:, 4, 0:L], cov, qf, start=True, stop=True).then_inc(s_ppe, 1)
                pe.wait_ge(s_pdve, b * NDV + 7)
                for t in range(QT):
                    pe.matmul(ps[:, 7, t * 32:t * 32 + H], zq[:, t * P:t * P + P], heads1[:], start=True, stop=True)
                    mm = pe.matmul(ps[:, 7, t * 32 + H:t * 32 + 2 * H], qf[:, t * P:t * P + P], mb,
                                   start=True, stop=True)
                mm.then_inc(s_ppe, 1)
            pe.wait_ge(s_pdve, B * NDV)

            def transposes_a(g, k):
                t = g * G + k
                pe.wait_ge(s_p, t + 1)
                if not isinstance(g, int) or g * G + k >= 1:
                    pe.wait_ge(s_cb, t)
                for c in range(8):
                    mm = pe.transpose(ps[:, 4 + c // 4, c % 4 * P:c % 4 * P + P],
                                      E[k % 2][:, c * P:c * P + P], ident[:])
                mm.then_inc(s_ta, 1)

            def transposes_b(g, k):
                t = g * G + k
                pe.wait_ge(s_ca, t + 1)
                for c in range(8, KC):
                    m = P if c < KC - 1 else KR
                    mm = pe.transpose(ps[0:m, 4 + (c - 8) // 4, c % 4 * P:c % 4 * P + P],
                                      E[k % 2][:, c * P:c * P + m], ident[:])
                mm.then_inc(s_tb, 1)

            def head(g, a):
                pe.wait_ge(s_cb, g * G + 2 * a + 2)
                pe.wait_ge(s_ca, g * G + 2 * a + 2)
                pe.wait_ge(s_vst, 2 * g + a + 1)
                if not isinstance(g, int) or 2 * g + a >= 1:
                    pe.wait_ge(s_ao, 2 * g + a)
                for c in range(KC):
                    m = P if c < KC - 1 else KR
                    mm = pe.matmul(ps[0:DH, 6, 0:L], vst[a][0:m, c, :], PT[a][0:m, c, :],
                                   start=(c == 0), stop=(c == KC - 1))
                mm.then_inc(s_av, 1)

            def scores(s, k):
                if k == 0:
                    pe.wait_ge(s_stk, 96 * (s + 1))
                slot = s % 2 * 2 + k // 2
                for piece in range(2):
                    if not isinstance(s, int) or s * G + k >= 1:
                        pe.wait_ge(s_ev, 2 * G * s + 2 * k - 1 + piece)
                    a, e = (0, CUT) if piece == 0 else (CUT, NK)
                    while a < e:
                        n = min(512, e - a)
                        mm = pe.matmul(psf[:, a:a + n], qst[:, bass.ds(slot, 1), k % 2 * P:k % 2 * P + P]
                                       .rearrange("p a q -> p (a q)"),
                                       kst[:, bass.ds(slot, 1), a:a + n].rearrange("p a k -> p (a k)"),
                                       start=True, stop=True)
                        a += n
                    mm.then_inc(s_sc, 1)

            scores(0, 0)

            def run(s, on):
                for k in range(G):
                    if on[0] and k < G - 1:
                        scores(s, k + 1)
                    if on[5] and k == G - 1:
                        scores(s + 1, 0)
                    if k == 0 and on[4]:
                        transposes_b(s - 4, G - 1)
                    if k > 0 and on[3]:
                        transposes_b(s - 3, k - 1)
                    if k == 1 and on[4]:
                        head(s - 4, 1)
                    if k == 3 and on[3]:
                        head(s - 3, 0)
                    if k == 3 and on[2]:
                        pe.wait_ge(s_badr, s - 1)
                        pe.matmul(ps[0:1, 7, 0:G], ones[:], bad[:], start=True, stop=True).then_inc(s_badc, 1)
                    if on[3]:
                        transposes_a(s - 3, k)
            steps(pe, run)

            pe.wait_ge(s_ew, 48)
            with pe.Fori(0, B * QT) as n:
                o, v, a = n * EPE, n * EDV, n * EAC
                pe.wait_ge(s_ein, 32 * (n + 1))
                pe.wait_ge(s_edve, v)
                pe.wait_ge(s_eact, a)
                pe.transpose(ps[:, 0, 0:P], ecT, ident[:]).then_inc(s_epe, 1)
                pe.wait_ge(s_edve, v + 1)
                pe.transpose(ps[:, 1, 0:P], ecn, ident[:]).then_inc(s_epe, 1)
                pe.wait_ge(s_eact, a + 1)
                pe.matmul(ps[:, 2, 0:D], ecnT, wo[:], start=True, stop=True).then_inc(s_epe, 1)
                pe.wait_ge(s_edve, v + 5)
                pe.transpose(ps[:, 3, 0:P], exn, ident[:]).then_inc(s_epe, 1)
                pe.wait_ge(s_eact, a + 3)
                pe.matmul(ps[:, 0, 0:NE], exnT, wr[:], start=True, stop=True).then_inc(s_epe, 1)
                pe.wait_ge(s_edve, v + 8)
                pe.transpose(ps[0:NE, 1, 0:P], eone, ident[:]).then_inc(s_epe, 1)
                pe.wait_ge(s_eact, a + 4)
                pe.matmul(ps[:, 2, :], eoneT[0:NE, :], b1s[0:NE, :], start=True,
                          stop=True).then_inc(s_epe, 1)
                for e in range(NE):
                    if e >= 4:
                        pe.wait_ge(s_edve, v + 8 + e - 3)
                    mm = pe.matmul(ps[:, 4 + e % 4, :], exnT, w1s[:, e, :], start=True, stop=True)
                    if e % 2:
                        mm.then_inc(s_epe, 1)
                pe.wait_ge(s_eact, a + 6)
                for c in range(NI // P):
                    mm = pe.transpose(ps[:, 1, c * P:c * P + P], egel[:, c * P:c * P + P], ident[:])
                mm.then_inc(s_epe, 1)
                pe.wait_ge(s_eact, a + 7)
                for c in range(NI // P):
                    mm = pe.matmul(ps[:, 3, 0:D], egT[:, c * P:c * P + P], wfs[:, c, :],
                                   start=(c == 0), stop=(c == NI // P - 1))
                mm.then_inc(s_epe, 2)

        @block.vector
        def _(dve):
            dve.wait_ge(s_const, 16 * NCONST)
            dve.wait_ge(s_cset, 1)

            def parts(src, res, out3):
                dve.tensor_copy(out3[0], src)
                dve.drain()
                dve.tensor_tensor(res, src, out3[0], ALU.subtract)
                dve.drain()
                dve.tensor_copy(out3[1], res)
                dve.drain()
                dve.tensor_tensor(res, res, out3[1], ALU.subtract)
                dve.drain()
                return dve.tensor_copy(out3[2], res)

            with dve.Fori(0, B) as b:
                o = b * NPE
                dve.wait_ge(s_pin, 64 * (b + 1))
                for t in range(QT):
                    dve.bn_stats(stats[:, t, :], xin[:, t, :])
                dve.drain()
                for t in range(QT):
                    ins = dve.bn_aggr(agg[:, t, :], stats[:, t, :])
                ins.then_inc(s_pst, 1)
                dve.wait_ge(s_pact, b * NAC + 1)
                dve.reciprocal(rstd, rstd)
                dve.drain()
                for t in range(QT):
                    ins = dve.tensor_scalar(xn[:, t, :], xin[:, t, :], agg[:, t, 0:1], rstd[:, t:t + 1],
                                            ALU.subtract, ALU.mult)
                ins.then_inc(s_pdve, 1)
                dve.wait_ge(s_ppe, o + 1)
                vps = psf[:, 4 * 512:4 * 512 + KC * P].rearrange("p (c d) -> p c d", c=KC)
                dve.tensor_tensor(V_all[:, 0:KC - 1, bass.ds(b * D, D)], vps[:, 0:KC - 1, :],
                                  bvb.unsqueeze(1).broadcast_to([P, KC - 1, D]), ALU.add)
                dve.tensor_tensor(V_all[0:KR, KC - 1, bass.ds(b * D, D)], vps[0:KR, KC - 1, :],
                                  bvb[0:KR, :], ALU.add).then_inc(s_pdve, 1)
                dve.wait_ge(s_ppe, o + 3)
                dve.tensor_scalar(gram, ps[:, 6, 0:D + 1], 1.0 / NK, None, ALU.mult).then_inc(s_pdve, 1)
                dve.wait_ge(s_ppe, o + 5)
                dve.tensor_copy(t1, ps[:, 7, 0:D])
                dve.tensor_copy(krow[0:1, :], ps[0:1, 7, D:2 * D])
                dve.tensor_scalar(nkrow[0:1, :], ps[0:1, 7, D:2 * D], -1.0, None, ALU.mult)
                dve.tensor_tensor(kb, ps[:, 7, 2 * D:2 * D + 1], bkc[:], ALU.add)
                dve.drain()
                dve.tensor_scalar(mb, heads1[:], kb, None, ALU.mult).then_inc(s_pdve, 1)
                dve.wait_ge(s_ppe, o + 6)
                dve.wait_ge(s_pout, b * 192)
                dve.tensor_scalar(qf, ps[:, 5, 0:L], bqc[:], QSCALE, ALU.add, ALU.mult)
                dve.drain()
                parts(qf, qres, qp).then_inc(s_pdve, 1)
                dve.wait_ge(s_ppe, o + 7)
                dve.tensor_tensor(cov, ps[:, 6, 0:D], blocks, ALU.mult).then_inc(s_pdve, 1)
                dve.wait_ge(s_ppe, o + 8)
                dve.tensor_tensor(zq, ps[:, 4, 0:L], qf, ALU.mult).then_inc(s_pdve, 1)
                dve.wait_ge(s_ppe, o + 9)
                st = ps[:, 7, 0:QT * 32].rearrange("p (t s) -> p t s", t=QT)
                dve.tensor_scalar(var, st[:, :, 0:H], 0.0, None, ALU.max).then_inc(s_pdve, 1)
                dve.wait_ge(s_pact, b * NAC + 4)
                c = bass.ds(b * H * QT, H * QT)
                by_t = lambda arr: arr[:, c].rearrange("p (h t) -> p t h", t=QT)
                dve.tensor_scalar(by_t(unit), sig, SLOPE, None, ALU.mult)
                dve.tensor_scalar(by_t(nthr), sig, -SHIFT, None, ALU.mult)
                dve.scalar_tensor_tensor(by_t(shift), sig, SHIFT, st[:, :, H:2 * H],
                                         ALU.mult, ALU.subtract).then_inc(s_pdve, 1)
                parts(kf, kres, kp).then_inc(s_pdve, 1)

            def select(g, k):
                t = g * G + k
                dve.wait_ge(s_cnt[3], t + 1)
                if k % 2 == 0:
                    dve.tensor_scalar(trial[:, k:k + 2], nthr[:, col(g * G + k, 2)], -1.0, None, ALU.mult)
                    dve.drain()
                sc = S_at(g % RING, k)
                dve.scalar_tensor_tensor(y[:], sc, trial[:, k:k + 1], sc, ALU.is_le, ALU.mult)
                dve.drain()
                for i in range(NSEG):
                    e = (i + 1) * SEG if i < NSEG - 1 else NK
                    dve.max(cand[:, k, 8 * i:8 * i + 8], y[:, i * SEG:e])
                dve.drain()

            def settle(g):
                c = col(g * G, G)
                n = NV - 1
                for i in range(3):
                    src = cand if i == 0 else cand2
                    for k in range(G):
                        dve.max(top[:, k, 8 * i:8 * i + 8], src[:, k, :])
                    dve.drain()
                    if i < 2:
                        for k in range(G):
                            dve.match_replace(cand2[:, k, :], top[:, k, 8 * i:8 * i + 8], src[:, k, :], 0.0)
                        dve.drain()
                dve.tensor_scalar(rank[:], sgn[:, c], -0.5, TOPK - NK / 2 + 0.25, ALU.mult, ALU.add)
                dve.tensor_reduce(seg8[:], cand[:, :, 7:8 * NSEG:8], AX.X, ALU.max)
                dve.drain()
                dve.tensor_scalar(rank[:], rank[:], 2.0 ** 23, -2.0 ** 23, ALU.add, ALU.add)
                dve.drain()
                dve.tensor_tensor(hit[:], ranks[:].unsqueeze(1).broadcast_to([P, G, n]),
                                  rank[:].unsqueeze(2).broadcast_to([P, G, n]), ALU.is_equal)
                dve.drain()
                dve.tensor_tensor(pick[:], hit[:], top[:, :, 0:n], ALU.mult)
                dve.drain()
                dve.tensor_reduce(thr[:, c], pick[:], AX.X, ALU.add)
                dve.drain()
                dve.tensor_tensor(pick[:], hit[:], top[:, :, 1:n + 1], ALU.mult)
                dve.drain()
                dve.tensor_reduce(nxt[:], pick[:], AX.X, ALU.add)
                dve.drain()
                dve.tensor_tensor(bad[:], seg8[:], thr[:, c], ALU.is_lt)
                dve.tensor_tensor(bad2[:], top[:, :, 1], trial[:], ALU.is_lt)
                dve.drain()
                dve.tensor_scalar(seg8[:], thr[:, c], 0.0, None, ALU.is_gt)
                dve.tensor_tensor(bad[:], bad[:], bad2[:], ALU.mult)
                dve.drain()
                dve.tensor_tensor(bad[:], bad[:], seg8[:], ALU.mult)
                dve.tensor_tensor(nxt[:], nxt[:], thr[:, c], ALU.is_equal)
                dve.drain()
                dve.tensor_scalar(bad[:], bad[:], -LOST, LOST, ALU.mult, ALU.add)
                dve.drain()
                dve.tensor_tensor(bad[:], bad[:], nxt[:], ALU.add).then_inc(s_badr, 1)

            def bisect(g, k):
                t = g * G + k
                sc = S_at(g % RING, k)
                top_s = nmax[:, col(t)]
                dve.tensor_scalar(y[:], sc, 1.0, None, ALU.mult, ALU.min, accum_out=lo[:])
                dve.tensor_scalar(mid[:], top_s, -1.0, None, ALU.mult)
                dve.drain()
                dve.tensor_tensor(hi[:], mid[:], lo[:], ALU.subtract)
                dve.tensor_tensor(w0[:], mid[:], top_s, ALU.max)
                dve.drain()
                dve.tensor_tensor(hi[:], hi[:], mid[:], ALU.add)
                dve.drain()
                dve.scalar_tensor_tensor(hi[:], hi[:], 1.0 / BIG, w0[:], ALU.add, ALU.add)
                dve.drain()
                with dve.Fori(0, BISECT):
                    dve.tensor_tensor(mid[:], lo[:], hi[:], ALU.add)
                    dve.drain()
                    dve.tensor_scalar(mid[:], mid[:], 0.5, None, ALU.mult)
                    dve.drain()
                    dve.tensor_scalar(y[:], sc, mid[:], None, ALU.is_ge, ALU.add, accum_out=cnt[:])
                    dve.drain()
                    dve.tensor_scalar(keep[:], cnt[:], TOPK - 0.5, None, ALU.is_ge)
                    dve.drain()
                    dve.tensor_scalar(w0[:], keep[:], 1.0, BIG, ALU.subtract, ALU.mult)
                    dve.tensor_tensor(w1[:], keep[:], mid[:], ALU.mult)
                    dve.drain()
                    dve.tensor_tensor(w0[:], w0[:], w1[:], ALU.add)
                    dve.tensor_tensor(w2[:], mid[:], w1[:], ALU.subtract)
                    dve.drain()
                    dve.tensor_tensor(lo[:], lo[:], w0[:], ALU.max)
                    dve.scalar_tensor_tensor(w2[:], keep[:], BIG, w2[:], ALU.mult, ALU.add)
                    dve.drain()
                    dve.tensor_tensor(hi[:], hi[:], w2[:], ALU.min)
                    dve.drain()

            def break_tie(g, k, above, under):
                t = g * G + k
                sc = S_at(g % RING, k)
                dve.tensor_scalar(y[:], sc, hi[:], None, above, ALU.add, accum_out=cnt[:])
                dve.drain()
                dve.tensor_scalar(keep[:], cnt[:], -1.0, float(TOPK), ALU.mult, ALU.add)
                dve.tensor_scalar(y[:], sc, lo[:], 0.5, ALU.is_ge, ALU.mult)
                dve.drain()
                dve.scalar_tensor_tensor(y[:], sc, hi[:], y[:], under, ALU.mult)
                dve.drain()
                dve.tensor_tensor_scan(y[:], y[:], y[:], 0.0, ALU.add, ALU.add)
                dve.drain()
                dve.tensor_scalar(y[:], y[:], keep[:], -BIG, ALU.is_gt, ALU.mult)
                dve.drain()
                dve.scalar_tensor_tensor(y[:], sc, hi[:], y[:], under, ALU.mult)
                dve.drain()
                dve.tensor_tensor(sc, sc, y[:], ALU.add)
                dve.tensor_copy(thr[:, col(t)], lo[:])
                dve.drain()

            def run(s, on):
                for k in range(G):
                    if on[0]:
                        t = s * G + k
                        for piece in range(2):
                            a, n = (0, CUT) if piece == 0 else (CUT, NK - CUT)
                            dve.wait_ge(s_sc, 2 * t + piece + 1)
                            dve.tensor_scalar(S_at(s % RING, k, a, n), psf[:, a:a + n], shift[:, col(t)], None,
                                              ALU.add, ALU.max, accum_out=mx[:, k, piece:piece + 1]
                                              ).then_inc(s_ev, 1)
                    if on[2]:
                        select(s - 2, k)
                    if k == 3 and on[2]:
                        settle(s - 2)
                    if on[3]:
                        g = s - 3
                        dve.wait_ge(s_exp, g * G + k + 1)
                        e = E[k % 2][:]
                        dve.scalar_tensor_tensor(e, S_at(g % RING, k), thr[:, col(g * G + k)], e,
                                                 ALU.is_ge, ALU.mult,
                                                 accum_out=Z[:, col(g * G + k)]).then_inc(s_p, 1)
                if on[0]:
                    dve.drain()
                    dve.tensor_tensor(nmax[:, col(s * G, G)], mx[:, :, 0], mx[:, :, 1], ALU.max)
                    dve.drain()
                    dve.tensor_scalar(nmax[:, col(s * G, G)], nmax[:, col(s * G, G)], -1.0, None, ALU.mult)
                if on[2]:
                    g = s - 2
                    dve.wait_ge(s_badc, g + 1)
                    dve.tensor_copy(badi[:, 0:G], ps[0:1, 7, 0:G])
                    dve.tensor_reduce(badf[:], ps[0:1, 7, 0:G], AX.X, ALU.add)
                    dve.drain()
                    dve.tensor_copy(badi[:, G:G + 1], badf[:])
                    dve.drain()
                    rows = dve.value_load(badi[0:1, G:G + 1], min_val=0, max_val=G * MOST)
                    with dve.If(rows > 0):
                        with dve.Fori(0, G) as k:
                            mine = dve.value_load(badi[0:1, bass.ds(k, 1)], min_val=0, max_val=MOST)
                            with dve.If(mine >= int(LOST)):
                                bisect(g, k)
                                break_tie(g, k, ALU.is_ge, ALU.is_lt)
                            with dve.Else():
                                with dve.If(mine > 0):
                                    dve.tensor_copy(lo[:], thr[:, col(g * G + k)])
                                    dve.tensor_copy(hi[:], thr[:, col(g * G + k)])
                                    dve.drain()
                                    break_tie(g, k, ALU.is_gt, ALU.is_le)
                    dve.drain().then_inc(s_sel, 1)
            steps(dve, run)

            dve.wait_ge(s_ew, 48)
            with dve.Fori(0, B * QT) as n:
                o, a = n * EPE, n * EAC

                def done(ins, n=1):
                    ins.then_inc(s_edve, n)

                def layernorm_stats(src):
                    dve.bn_stats(est, src)
                    dve.drain()
                    done(dve.bn_aggr(eag, est))

                dve.wait_ge(s_ein, 32 * (n + 1))
                dve.wait_ge(s_out, 16 * n)
                zs = Z[:, bass.ds(n // QT * H * QT, H * QT)].rearrange("p (h t) -> p t h", t=QT)
                dve.reciprocal(erz, zs[:, bass.ds(n % QT, 1), :].rearrange("p a h -> p (a h)"))
                dve.drain()
                dve.wait_ge(s_epe, o + 1)
                done(dve.tensor_tensor(ecn.rearrange("p (h d) -> p h d", h=H),
                                       ps[:, 0, 0:D].rearrange("p (h d) -> p h d", h=H),
                                       erz.unsqueeze(2).broadcast_to([P, H, DH]), ALU.mult))
                dve.wait_ge(s_epe, o + 3)
                done(dve.tensor_tensor(ex1, ps[:, 2, 0:D], bob[:], ALU.add))
                dve.drain()
                done(dve.tensor_tensor(ex1, ex1, ex, ALU.add))
                dve.drain()
                layernorm_stats(ex1)
                dve.wait_ge(s_eact, a + 2)
                dve.reciprocal(ers, ers)
                dve.drain()
                done(dve.tensor_scalar(exn, ex1, eag[:, 0:1], ers, ALU.subtract, ALU.mult))
                dve.wait_ge(s_epe, o + 5)
                done(dve.tensor_reduce(emx, ps[:, 0, 0:NE], AX.X, ALU.max))
                dve.drain()
                dve.tensor_scalar(elog, ps[:, 0, 0:NE], emx, None, ALU.is_equal)
                dve.drain()
                done(dve.tensor_tensor(elog, elog, firsts[:], ALU.mult))
                dve.drain()
                dve.tensor_reduce(emx, elog, AX.X, ALU.max)
                dve.drain()
                done(dve.tensor_scalar(eone, elog, emx, None, ALU.is_equal))
                dve.drain()
                dve.wait_ge(s_eact, a + 5)
                for e in range(NE):
                    if e % 2 == 0:
                        dve.wait_ge(s_epe, o + 8 + e // 2)
                    done(dve.scalar_tensor_tensor(eacc, ps[:, 4 + e % 4, :], eone[:, e:e + 1], eacc,
                                                  ALU.mult, ALU.add))
                    dve.drain()
                dve.wait_ge(s_epe, o + 14)
                dve.tensor_tensor(ey, ps[:, 3, 0:D], bfb[:], ALU.add)
                dve.drain()
                done(dve.tensor_tensor(ey, ey, exn, ALU.add))
                dve.drain()
                layernorm_stats(ey)
                dve.wait_ge(s_eact, a + 8)
                dve.reciprocal(ers, ers)
                dve.drain()
                dve.tensor_scalar(ey, ey, eag[:, 0:1], ers, ALU.subtract, ALU.mult)
                dve.drain()
                dve.tensor_tensor(ey, ey, gab[:], ALU.mult)
                dve.drain()
                dve.tensor_tensor(ey, ey, beb[:], ALU.add)
                dve.drain()
                done(dve.tensor_tensor(eout, ey, ex1, ALU.add))


def kernel(**inputs):
    import concourse.bacc as bacc
    from concourse.bass_utils import run_bass_kernel_spmd as run

    nc = bacc.Bacc("TRN2", target_bir_lowering=False, num_devices=1)
    a = {k: np.asarray(v) for k, v in inputs.items()}
    head_of = np.arange(P) // DH
    arrays = {
        "x": a["x"].reshape(B * L, D),
        "ctx": a["ctx_1024"].reshape(B * NK, D),
        "ctxT": a["ctx_1024"].transpose(0, 2, 1).reshape(B * D, NK),
        "WqT": a["L0_xattn_Wq"].T, "bq": a["L0_xattn_bq"],
        "WkT": a["L0_xattn_Wk"].T, "bk": a["L0_xattn_bk"],
        "WvT": a["L0_xattn_Wv"].T, "bv": a["L0_xattn_bv"],
        "WoT": a["L0_xattn_Wo"].T, "bo": a["L0_xattn_bo"],
        "WrT": a["L0_ffn_Wr"].T, "W1": a["L0_ffn_W1"], "b1": a["L0_ffn_b1"],
        "Wf": a["L0_ffn_Wo"], "bf": a["L0_ffn_bo"],
        "gamma": a["L0_ffn_gamma"], "beta": a["L0_ffn_beta"],
        "ident": np.eye(P, dtype=np.float32),
        "blocks": (head_of[:, None] == head_of[None, :]).astype(np.float32),
        "heads": (head_of[:, None] == np.arange(H)[None, :]).astype(np.float32),
        "ranks": np.tile(np.arange(1, NV, dtype=np.float32), (P, 1)),
        "firsts": np.tile(np.arange(NE, 0, -1, dtype=np.float32), (P, 1)),
    }
    args = []
    for name in arrays:
        arrays[name] = np.ascontiguousarray(arrays[name])
        args.append(nc.dram_tensor(f"in_{name}", arrays[name].shape, F32, kind="ExternalInput").ap())
    args.append(nc.dram_tensor("out", (B * L, D), F32, kind="ExternalOutput").ap())
    build(nc, *args)
    r = run(nc, [{f"in_{k}": v for k, v in arrays.items()}], core_ids=[0])
    return r.results[0]["out"].reshape(B, L, D)
```

```python
from contextlib import ExitStack

import numpy as np
import concourse.bass as bass
from concourse import mybir

F32 = mybir.dt.float32
BF16 = mybir.dt.bfloat16
I32 = mybir.dt.int32
ALU = mybir.AluOpType
ACT = mybir.ActivationFunctionType
AX = mybir.AxisListType

P = 128
B, L, D = 4, 256, 128
NK = 1601
H, DH = 16, 8
TOPK = NK // 2
NI, NE = 512, 8
KC = 13
KR = NK - (KC - 1) * P
QT = L // P
G = 2 * QT
NG = B * H * QT // G
NT = B * H * QT
RING = 4
CUT = 1024
PART = DH * 3

NSEG = 8
SEG = NK // NSEG
NV = 24
AIM = 8
LAST_AIM = 9
LEAN = 0.2
SHIFT = 1.0
SLOPE = 1.0 / (2 * NK * 0.4)
STIFF = 600.0
BISECT = 48
BIG = 1e30
LOST = 1024.0
MOST = P * (int(LOST) + 1)
QSCALE = float(1.0 / np.sqrt(DH))


def build(nc, x, ctx, ctxT, WqT, bq, WkT, bk, WvT, bv, WoT, bo, WrT, W1, b1, Wf, bf, gamma, beta,
          ident_in, blocks_in, heads_in, ranks_in, firsts_in, picks_in, out):
    with ExitStack() as es:
        def sb(name, shape, dt=F32):
            return es.enter_context(nc.sbuf_tensor(name, shape, dt))

        def sem(name):
            return es.enter_context(nc.semaphore(name))

        k_parts = nc.dram_tensor("k_parts", [B * H * PART, NK], BF16).ap()
        q_parts = [nc.dram_tensor(f"q_parts{g}", [B * H * PART, L], BF16).ap() for g in range(3)]
        heads_T = nc.dram_tensor("heads_T", [B * H * DH, L], F32).ap()

        S = sb("S", [P, RING * G * NK])
        y = sb("y", [P, NK])
        E = [sb(f"E{i}", [P, NK]) for i in range(2)]
        signs = sb("signs", [P, G, NK], mybir.dt.int8)
        kst_flat = sb("kst", [P, 4 * NK], BF16)
        kst = kst_flat[:].rearrange("p (a k) -> p a k", a=4)
        qst = sb("qst", [P, 4, L], BF16)
        PT = [sb(f"PT{i}", [P, KC, L]) for i in range(2)]
        V_all = sb("V_all", [P, KC, B * D])
        vst = [sb(f"vst{i}", [P, KC, DH]) for i in range(2)]
        osb = [sb(f"osb{i}", [DH, L]) for i in range(2)]
        cand = sb("cand", [P, G, NSEG * 8])
        cand2 = sb("cand2", [P, G, NSEG * 8])
        top = sb("top", [P, G, NV])
        hit = sb("hit", [P, G, NV - 1])
        pick = sb("pick", [P, G, NV - 1])
        trial = sb("trial", [P, G])
        rank = sb("rank", [P, G])
        nxt = sb("nxt", [P, G])
        seg8 = sb("seg8", [P, G])
        bad = sb("bad", [P, G])
        bad2 = sb("bad2", [P, G])
        badf = sb("badf", [1, 1])
        badi = sb("badi", [1, G + 1], I32)
        mx = sb("mx", [P, G, 2])
        shift = sb("shift", [P, NT])
        unit = sb("unit", [P, NT])
        nthr = sb("nthr", [P, NT])
        thr = sb("thr", [P, NT])
        nmax = sb("nmax", [P, NT])
        sgn = sb("sgn", [P, NT])
        fprev = sb("fprev", [P, NT])
        step_c = sb("step_c", [P, NT])
        ratio = sb("ratio", [P, NT])
        Z = sb("Z", [P, NT])
        c_aim = sb("c_aim", [P, G // 2])
        c_one = sb("c_one", [P, G // 2])
        c_stiff = sb("c_stiff", [P, G // 2])
        c_neg = sb("c_neg", [P, G // 2])
        g_wait, a_wait = sb("g_wait", [P, G // 2]), sb("a_wait", [P, 2])
        g_f = sb("g_f", [P, G // 2])
        g_df = sb("g_df", [P, G // 2])
        g_num = sb("g_num", [P, G // 2])
        g_old = sb("g_old", [P, G // 2])
        g_den = sb("g_den", [P, G // 2])
        g_r = sb("g_r", [P, G // 2])
        g_e = sb("g_e", [P, G // 2])
        g_d = sb("g_d", [P, G // 2])
        lo, hi, mid, cnt, keep, w0, w1, w2 = (sb(n, [P, 1]) for n in ("lo", "hi", "mid", "cnt", "keep", "w0", "w1", "w2"))
        ident = sb("ident", [P, P])
        heads1 = sb("heads1", [P, H])
        ranks = sb("ranks", [P, NV - 1])
        firsts = sb("firsts", [P, NE])
        ones = sb("ones", [P, 1])
        wo = sb("wo", [P, D])
        wr = sb("wr", [P, NE])
        bqc, bkc = sb("bqc", [P, 1]), sb("bkc", [P, 1])
        bob, bfb, gab, beb = (sb(n, [P, D]) for n in ("bob", "bfb", "gab", "beb"))
        eps5, eps12 = sb("eps5", [P, 1]), sb("eps12", [P, 1])

        ps = es.enter_context(nc.psum_tensor("ps", [P, 8, 512], F32))
        psf = ps[:].rearrange("p a b -> p (a b)")

        used = [0]

        def carve(n, dt=F32):
            a = S[:, used[0]:used[0] + n]
            used[0] += n
            if dt == BF16:
                a = a.bitcast(BF16)
            return a

        wq, wk, wv, bvb, blocks = (carve(D) for _ in range(5))
        cT = carve(NK)
        cx = carve(KC * (D + 1)).rearrange("p (c d) -> p c d", c=KC)
        kf = carve(NK)
        kres = carve(NK)
        kp = [carve(NK // 2 + 1, BF16)[:, 0:NK] for _ in range(3)]
        xin = carve(QT * D).rearrange("p (t d) -> p t d", t=QT)
        xn = carve(QT * D).rearrange("p (t d) -> p t d", t=QT)
        xnT = carve(L)
        qf = carve(L)
        qres = carve(L)
        qp = [carve(L // 2, BF16) for _ in range(3)]
        gram = carve(D + 1)
        t1 = carve(D)
        krow = carve(D)
        nkrow = carve(D)
        cov = carve(D)
        mb = carve(H)
        kb = carve(1)
        zq = carve(L)
        var = carve(QT * H).rearrange("p (t h) -> p t h", t=QT)
        sig = carve(QT * H).rearrange("p (t h) -> p t h", t=QT)
        stats = carve(QT * 6).rearrange("p (t s) -> p t s", t=QT)
        agg = carve(QT * 2).rearrange("p (t s) -> p t s", t=QT)
        rstd = carve(QT)
        assert used[0] <= RING * G * NK

        T = QT * P

        def carve_from(slot):
            used[0] = slot * G * NK

        def each(n, m=B):
            return [carve(n) for _ in range(m)]

        def tiles(arr):
            return [a.rearrange("p (t d) -> p t d", t=QT) for a in arr]

        carve_from(0)
        xb = each(T)
        ecT, ecn, ecnT, x1, xn2, xnT2 = (each(T, 2) for _ in range(6))
        xm = each(T, 2)
        rz, estd, emx = each(QT * H), each(QT), each(QT)
        est, eag, elog, eone = (tiles(each(QT * n)) for n in (6, 2, NE, NE))
        b1s = carve(NI)
        assert used[0] <= G * NK
        carve_from(1)
        for a in (ecT, ecn, ecnT, x1, xn2, xnT2):
            a += each(T, 2)
        wfs = carve(NI // P * D).rearrange("p (c d) -> p c d", c=NI // P)
        hT = [carve(NI * QT).rearrange("p (c q) -> p c q", c=NI // P) for _ in range(2)]
        assert used[0] <= 2 * G * NK
        carve_from(2)
        hT += [carve(NI * QT).rearrange("p (c q) -> p c q", c=NI // P) for _ in range(2)]
        xnb, x1b, ey = (each(T) for _ in range(3))
        assert used[0] <= 3 * G * NK
        assert NE + (NE + 2) // 3 < KC and NI == 4 * P and B == 4

        def w1_at(e, c):
            return (V_all[:, e, c * P:c * P + P] if c < 3 else
                    V_all[:, NE + e // 3, e % 3 * P:e % 3 * P + P])

        kfree = kst_flat[:].bitcast(F32)
        picks = kfree[0:NE, 0:NE * P]
        oneT = [kfree[0:NE, NE * P + b * T:NE * P + b * T + T] for b in range(B)]
        used_b = 2 * (NE * P + B * T)
        picks_b = kst_flat[0:NE, used_b:used_b + NE * P]
        used_b += NE * P
        oneT_b = [kst_flat[0:NE, used_b + b * T:used_b + b * T + T] for b in range(B)]
        assert used_b + B * T <= 4 * NK

        s_const = sem("s_const")
        s_cset = sem("s_cset")
        s_pin = sem("s_pin")
        s_ppe = sem("s_ppe")
        s_pdve = sem("s_pdve")
        s_pst = sem("s_pst")
        s_pact = sem("s_pact")
        s_pout = sem("s_pout")
        s_stk = sem("s_stk")
        s_sc = sem("s_sc")
        s_ev = sem("s_ev")
        s_nm = sem("s_nm")
        s_cnt = [sem(f"s_cnt{i}") for i in range(4)]
        s_thr = [sem(f"s_thr{i}") for i in range(4)]
        s_badr = sem("s_badr")
        s_badc = sem("s_badc")
        s_sel = sem("s_sel")
        s_exp = sem("s_exp")
        s_p = sem("s_p")
        s_ta = sem("s_ta")
        s_tb = sem("s_tb")
        s_ca = sem("s_ca")
        s_cb = sem("s_cb")
        s_vst = sem("s_vst")
        s_av = sem("s_av")
        s_ao = sem("s_ao")
        s_aw = [sem(f"s_aw{a}") for a in range(2)]
        s_ein = [sem(f"s_ein{h}") for h in range(B)]
        s_ex = sem("s_ex")
        s_ew = sem("s_ew")
        s_epk = sem("s_epk")
        s_epb = sem("s_epb")
        s_exb = sem("s_exb")
        s_hq = sem("s_hq")
        s_hn = sem("s_hn")
        s_hb = sem("s_hb")
        s_hc = sem("s_hc")
        s_wo = sem("s_wo")
        s_x1 = sem("s_x1")
        s_st1 = sem("s_st1")
        s_sd1 = sem("s_sd1")
        s_xn = sem("s_xn")
        s_xt = sem("s_xt")
        s_xc = sem("s_xc")
        s_rt = sem("s_rt")
        s_one = sem("s_one")
        s_ot = sem("s_ot")
        s_oc = sem("s_oc")
        s_mk = sem("s_mk")
        s_xm = sem("s_xm")
        s_xu = sem("s_xu")
        s_gl = sem("s_gl")
        s_dn = sem("s_dn")
        s_ads = sem("s_ads")
        s_st2 = sem("s_st2")
        s_sd2 = sem("s_sd2")
        s_fin = sem("s_fin")
        s_out = sem("s_out")

        NCONST = 17
        NPE, NDV, NAC = 9, 10, 4

        ps_bad = ps[0:1, 7, 0:G]
        CHAIN = [2, 3, 2, 5]

        def ps_chain(b):
            return ps[:, CHAIN[b], 0:T]

        def ps_up(b, c):
            return ps[:, b % 2 * 2 + c // 2, c % 2 * T:c % 2 * T + T]

        def ps_down(b):
            return ps[:, b % 2 * 2, 0:T]

        ps_mask = ps[:, 7, 0:T]

        def S_at(slot, k, a=0, n=NK):
            return S[:, bass.ds((slot * G + k) * NK + a, n)]

        def col(t, n=1):
            return bass.ds(t, n)

        def steps(eng, run):
            def stages(s):
                return [0 <= s - i < NG for i in range(5)] + [s + 1 < NG]
            for s in range(4):
                run(s, stages(s))
            with eng.Fori(4, NG - 1) as s:
                run(s, [True] * 6)
            for s in range(NG - 1, NG + 4):
                run(s, stages(s))

        block = es.enter_context(nc.Block())

        @block.sync
        def _(sp):
            consts = [(ident, ident_in), (blocks, blocks_in), (heads1, heads_in), (ranks, ranks_in), (firsts, firsts_in),
                      (wq, WqT), (wk, WkT), (wv, WvT), (wo, WoT), (wr, WrT),
                      (bqc, bq.rearrange("(p a) -> p a", a=1)), (bkc, bk.rearrange("(p a) -> p a", a=1))]
            for dst, src in consts:
                sp.dma_start(dst[:, :], src).then_inc(s_const, 16)
            for dst, src in ((bvb, bv), (bob, bo), (bfb, bf), (gab, gamma), (beb, beta)):
                sp.dma_start(dst[:, :], src.rearrange("(a d) -> a d", a=1).broadcast_to([P, D])).then_inc(s_const, 16)
            sp.wait_ge(s_cset, 1)
            full = (KC - 1) * P
            with sp.Fori(0, B) as b:
                sp.wait_ge(s_pdve, b * NDV)
                sp.dma_start(cT, ctxT[bass.ds(b * D, D), :]).then_inc(s_pin, 16)
                sp.dma_start(cx[:, 0:KC - 1, 0:D],
                             ctx[bass.ds(b * NK, full), :].rearrange("(c p) d -> p c d", p=P)).then_inc(s_pin, 16)
                sp.dma_start(cx[0:KR, KC - 1, 0:D], ctx[bass.ds(b * NK + full, KR), :]).then_inc(s_pin, 16)
                sp.dma_start(xin, x[bass.ds(b * L, L), :].rearrange("(t p) d -> p t d", p=P)).then_inc(s_pin, 16)
                sp.wait_ge(s_pdve, b * NDV + 5)
                for g in range(3):
                    dst = q_parts[g][bass.ds(b * H * PART, H * PART), :].rearrange("(r j) q -> r j q", j=3)
                    for j in range(3):
                        sp.dma_start(dst[:, j, :], qp[g]).then_inc(s_pout, 16)
                sp.wait_ge(s_pdve, b * NDV + 10)
                dst = k_parts[bass.ds(b * H * PART, H * PART), :].rearrange("(r j) k -> r j k", j=3)
                for j in range(3):
                    sp.dma_start(dst[:, j, :], kp[j]).then_inc(s_pout, 16)
            sp.wait_ge(s_pout, B * 12 * 16)

            def stacked(s):
                if not isinstance(s, int) or s >= 2:
                    sp.wait_ge(s_sc, 2 * G * (s - 1))
                if not isinstance(s, int) or s >= 1:
                    sp.wait_ge(s_stk, 96 * s)
                slot = s % 2 * 2
                for g in range(3):
                    sp.dma_start(kst[32 * g:32 * g + PART, bass.ds(slot, 2), :],
                                 k_parts[bass.ds(s * 2 * PART, 2 * PART), :]
                                 .rearrange("(a r) k -> r a k", a=2)).then_inc(s_stk, 16)
                    sp.dma_start(qst[32 * g:32 * g + PART, bass.ds(slot, 2), :],
                                 q_parts[g][bass.ds(s * 2 * PART, 2 * PART), :]
                                 .rearrange("(a r) k -> r a k", a=2)).then_inc(s_stk, 16)

            stacked(0)

            def epilogue_loads(s):
                if s == NG - 1:
                    for a in range(2):
                        sp.wait_ge(s_aw[a], 16 * (NG // B) * (B - 1))
                    sp.wait_ge(s_vst, (B - 1) * H)
                    sp.dma_start(V_all[:, 0:NE, 0:3 * P], W1[:, :, 0:3 * P].rearrange("e d n -> d e n")).then_inc(s_ew, 16)
                    for e in range(0, NE, 3):
                        n = min(3, NE - e)
                        sp.dma_start(V_all[:, NE + e // 3, 0:n * P].rearrange("p (e n) -> p e n", e=n),
                                     W1[e:e + n, :, 3 * P:].rearrange("e d n -> d e n")).then_inc(s_ew, 16)
                if s == NG:
                    sp.wait_ge(s_p, G * (NG - RING + 1))
                    for b in range(2):
                        sp.dma_start(ecT[b], heads_T[b * D:b * D + D, :]).then_inc(s_ein[b], 16)
                    for b in range(B):
                        sp.dma_start(xb[b].rearrange("p (n d) -> p n d", n=QT),
                                     x[b * T:b * T + T, :].rearrange("(n p) d -> p n d", p=P)).then_inc(s_ex, 16)
                    sp.dma_start(b1s[0:NE, :], b1).then_inc(s_ew, 16)
                    sp.wait_ge(s_sc, 2 * NT)
                    sp.dma_start(picks, picks_in).then_inc(s_epk, 16)
                if s == NG + 1:
                    sp.wait_ge(s_p, G * (NG - RING + 2))
                    sp.dma_start(ecT[2], heads_T[2 * D:3 * D, :]).then_inc(s_ein[2], 16)
                    sp.dma_start(wfs, Wf.rearrange("(c p) d -> p c d", p=P)).then_inc(s_ew, 16)

            def run(s, on):
                if on[5]:
                    stacked(s + 1)
                else:
                    epilogue_loads(s)
                if on[4]:
                    sp.wait_ge(s_ao, 2 * (s - 4) + 2)
                    sp.dma_start(heads_T[bass.ds((s - 4) * 2 * DH + DH, DH), :], osb[1][:]).then_inc(s_aw[1], 16)
                if on[3]:
                    sp.wait_ge(s_ao, 2 * (s - 3) + 1)
                    sp.dma_start(heads_T[bass.ds((s - 3) * 2 * DH, DH), :], osb[0][:]).then_inc(s_aw[0], 16)
            steps(sp, run)

            for a in range(2):
                sp.wait_ge(s_aw[a], 16 * NG)
            sp.dma_start(ecT[3], heads_T[3 * D:4 * D, :]).then_inc(s_ein[3], 16)
            for b in range(B):
                sp.wait_ge(s_fin, b + 1)
                sp.dma_start(out[b * T:b * T + T, :].rearrange("(n p) d -> p n d", p=P),
                             ey[b].rearrange("p (n d) -> p n d", n=QT)).then_inc(s_out, 16)
            sp.wait_ge(s_out, 16 * B)

        @block.gpsimd
        def _(pool):
            pool.memset(kst_flat[:], 0.0)
            pool.memset(qst[:], 0.0)
            pool.memset(ones[:], 1.0)
            pool.memset(eps5[:], 1e-5)
            pool.memset(eps12[:], 1e-12)
            pool.memset(cx[:, :, D:D + 1], 1.0)
            pool.memset(c_aim[:], float(NK - 2 * (TOPK - AIM)))
            pool.memset(c_one[:], 1.0)
            pool.memset(c_stiff[:], STIFF)
            pool.memset(c_neg[:], -1.0)
            pool.memset(ratio[:], 1.0)
            pool.drain().then_inc(s_cset, 1)

            def correct(g, r, h):
                c = col(g * G + h * G // 2, G // 2)
                pool.wait_ge(s_cnt[r], G * g + (h + 1) * G // 2)
                pool.tensor_tensor(g_wait[:], c_one[:], c_one[:], ALU.mult)
                pool.tensor_tensor(g_f[:], sgn[:, c], c_aim[:], ALU.add)
                pool.drain()
                if r > 0:
                    pool.tensor_tensor(g_df[:], fprev[:, c], g_f[:], ALU.subtract)
                    pool.tensor_tensor(g_old[:], ratio[:, c], c_stiff[:], ALU.mult)
                    pool.drain()
                    pool.tensor_tensor(g_num[:], step_c[:, c], g_df[:], ALU.mult)
                    pool.tensor_tensor(g_den[:], g_df[:], g_df[:], ALU.mult)
                    pool.drain()
                    pool.tensor_tensor(g_num[:], g_num[:], g_old[:], ALU.add)
                    pool.tensor_tensor(g_den[:], g_den[:], c_stiff[:], ALU.add)
                    pool.drain()
                    pool.tensor_tensor(g_den[:], g_den[:], c_neg[:], ALU.pow)
                    pool.drain()
                    pool.tensor_tensor(g_r[:], g_num[:], g_den[:], ALU.mult)
                    pool.drain()
                    pool.tensor_scalar(g_r[:], g_r[:], 0.4, 2.2, ALU.max, ALU.min)
                    pool.drain()
                    pool.tensor_tensor(g_d[:], g_f[:], g_r[:], ALU.mult)
                else:
                    pool.tensor_tensor(g_d[:], g_f[:], c_one[:], ALU.mult)
                if r < 2:
                    pool.tensor_tensor(fprev[:, c], g_f[:], c_one[:], ALU.mult)
                    if r > 0:
                        pool.tensor_tensor(ratio[:, c], g_r[:], c_one[:], ALU.mult)
                    pool.drain()
                    pool.tensor_tensor(step_c[:, c], g_d[:], c_one[:], ALU.mult)
                else:
                    pool.drain()
                    pool.tensor_scalar(g_num[:], g_d[:], 0.0, 2 * LEAN, ALU.max, ALU.mult)
                    pool.tensor_scalar(g_den[:], g_d[:], 1 - LEAN, 2.0 * (LAST_AIM - AIM), ALU.mult, ALU.add)
                    pool.drain()
                    pool.tensor_tensor(g_d[:], g_num[:], g_den[:], ALU.add)
                    pool.drain()
                pool.tensor_tensor(g_e[:], g_d[:], unit[:, c], ALU.mult)
                pool.drain()
                pool.tensor_tensor(nthr[:, c], nthr[:, c], g_e[:], ALU.subtract).then_inc(s_thr[r + 1], 1)

            def lay_v(g, a):
                if not isinstance(g, int) or g >= 1:
                    pool.wait_ge(s_av, 2 * g - 1 + a)
                pool.tensor_copy(vst[a][:, 0:KC - 1, :],
                                 V_all[:, 0:KC - 1, bass.ds(g * 2 * DH + a * DH, DH)])
                pool.tensor_copy(vst[a][0:KR, KC - 1, :],
                                 V_all[0:KR, KC - 1, bass.ds(g * 2 * DH + a * DH, DH)]).then_inc(s_vst, 1)

            pool.wait_ge(s_pdve, B * NDV)

            def run(s, on):
                if on[1]:
                    for h in range(2):
                        correct(s - 1, 0, h)
                if on[3]:
                    lay_v(s - 3, 0)
                if not on[0] and s == NG:
                    pool.wait_ge(s_ex, 16 * B)
                    for h in range(B):
                        pool.tensor_tensor(xb[h].rearrange("p (n d) -> p n d", n=QT),
                                           xb[h].rearrange("p (n d) -> p n d", n=QT),
                                           bob[:].unsqueeze(1).broadcast_to([P, QT, D]), ALU.add).then_inc(s_exb, 1)
                if on[1]:
                    for r in range(1, 3):
                        for h in range(2):
                            correct(s - 1, r, h)
                if on[3]:
                    lay_v(s - 3, 1)
                if not on[0] and s == NG:
                    pool.wait_ge(s_epk, 16)
                    pool.tensor_copy(picks_b, picks).then_inc(s_epb, 1)
            steps(pool, run)

            pool.wait_ge(s_p, G * (NG - RING + 3))
            for h in range(B):
                pool.wait_ge(s_xn, h + 1)
                for dst, src, vec in ((xnb, xn2, bfb), (x1b, x1, beb)):
                    pool.tensor_tensor(dst[h].rearrange("p (n d) -> p n d", n=QT),
                                       src[h].rearrange("p (n d) -> p n d", n=QT),
                                       vec[:].unsqueeze(1).broadcast_to([P, QT, D]), ALU.add).then_inc(s_ads, 1)

        @block.scalar
        def _(act):
            with act.Fori(0, B) as b:
                act.wait_ge(s_pst, b + 1)
                act.activation(rstd, agg[:, :, 1], ACT.Sqrt, bias=eps5[:]).then_inc(s_pact, 1)
                act.wait_ge(s_pdve, b * NDV)
                act.wait_ge(s_ppe, b * NPE + 2)
                act.activation(kf, psf[:, 0:NK], ACT.Identity, bias=bkc[:]).then_inc(s_pact, 1)
                act.wait_ge(s_ppe, b * NPE + 4)
                act.activation(xnT, ps[:, 4, 0:L], ACT.Copy).then_inc(s_pact, 1)
                act.wait_ge(s_pdve, b * NDV + 8)
                act.activation(sig, var, ACT.Sqrt).then_inc(s_pact, 1)
            act.wait_ge(s_pdve, B * NDV)

            def count(g, r, k):
                t = g * G + k
                if r == 0:
                    if k == 0 and (not isinstance(g, int) or g >= 1):
                        act.wait_ge(s_cnt[3], G * g)
                    act.wait_ge(s_ev, 2 * G * g + 2 * k + 2)
                elif k % 2 == 0:
                    act.wait_ge(s_thr[r], 2 * g + k // 2 + 1)
                    act.activation(a_wait[:, k // 2:k // 2 + 1], ones[:], ACT.Copy)
                act.activation(signs[:, k, :], S_at(g % RING, k), ACT.Sign, bias=nthr[:, col(t)],
                               accum_out=sgn[:, col(t)]).then_inc(s_cnt[r], 1)

            def copy_a(g, k):
                act.wait_ge(s_ta, g * G + k + 1)
                if k % 2 == 0 and (not isinstance(g, int) or g >= 1):
                    act.wait_ge(s_av, 2 * g - 1 + k // 2)
                for i in range(2):
                    ins = act.activation(PT[k // 2][:, 4 * i:4 * i + 4, k % 2 * P:k % 2 * P + P],
                                         ps[:, 4 + i, :].rearrange("p (c q) -> p c q", c=4), ACT.Copy)
                ins.then_inc(s_ca, 1)

            def copy_b(g, k):
                act.wait_ge(s_tb, g * G + k + 1)
                q = slice(k % 2 * P, k % 2 * P + P)
                act.activation(PT[k // 2][:, 8:12, q], ps[:, 4, :].rearrange("p (c q) -> p c q", c=4), ACT.Copy)
                act.activation(PT[k // 2][0:KR, 12, q], ps[0:KR, 5, 0:P], ACT.Copy).then_inc(s_cb, 1)

            def head_out(g, a):
                act.wait_ge(s_av, 2 * g + a + 1)
                if not isinstance(g, int) or g >= 1:
                    act.wait_ge(s_aw[a], 16 * g)
                act.activation(osb[a][:], ps[0:DH, 6, 0:L], ACT.Copy).then_inc(s_ao, 1)

            def heads_back(h):
                act.wait_ge(s_hb, h + 1)
                act.activation(ecnT[h], ps_chain(h), ACT.Copy).then_inc(s_hc, 1)

            def deviation(h):
                act.wait_ge(s_st1, h + 1)
                act.activation(estd[h], eag[h][:, :, 1], ACT.Sqrt, bias=eps5[:]).then_inc(s_sd1, 1)

            def normed_T(h):
                act.wait_ge(s_xt, h + 1)
                act.activation(xnT2[h], ps_chain(h), ACT.Copy).then_inc(s_xc, 1)

            def choice_T(h):
                act.wait_ge(s_ot, h + 1)
                act.activation(oneT_b[h], ps_chain(h)[0:NE, :], ACT.Copy)
                act.activation(oneT[h], ps_chain(h)[0:NE, :], ACT.Copy).then_inc(s_oc, 1)

            def gelu(h):
                act.wait_ge(s_xu, NE * (h + 1))
                for c in range(NI // P):
                    act.activation(hT[h][:, c, :], ps_up(h, c), ACT.Gelu).then_inc(s_gl, 1)

            def last_deviation(h):
                act.wait_ge(s_st2, h + 1)
                act.activation(estd[h], eag[h][:, :, 1], ACT.Sqrt, bias=eps12[:]).then_inc(s_sd2, 1)

            def early_parts(s, k):
                if (s, k) == (NG, 1):
                    heads_back(0)
                    heads_back(1)
                if (s, k) == (NG, 2):
                    deviation(0)
                    deviation(1)
                if (s, k) == (NG, 3):
                    normed_T(0)
                    normed_T(1)
                if (s, k) == (NG + 1, 0):
                    choice_T(0)
                    choice_T(1)
                if (s, k) == (NG + 1, 2):
                    heads_back(2)
                if (s, k) == (NG + 1, 3):
                    deviation(2)
                if (s, k) == (NG + 2, 0):
                    normed_T(2)
                    choice_T(2)
                if (s, k) == (NG + 2, 3):
                    gelu(0)
                if (s, k) == (NG + 3, 2):
                    gelu(1)

            def run(s, on):
                for k in range(G):
                    if on[1]:
                        count(s - 1, k, 0)
                        count(s - 1, k, 1)
                    if on[3]:
                        t = (s - 3) * G + k
                        if k == 0:
                            act.wait_ge(s_sel, s - 2)
                        if k >= 2 or not isinstance(s, int) or s > 3:
                            act.wait_ge(s_tb, t - 1)
                        act.activation(E[k % 2][:], S_at((s - 3) % RING, k), ACT.Exp,
                                       bias=nmax[:, col(t)]).then_inc(s_exp, 1)
                    if k > 0 and on[3]:
                        copy_a(s - 3, k - 1)
                    if k == 0 and on[4]:
                        copy_a(s - 4, G - 1)
                    if k == 2 and on[4]:
                        head_out(s - 4, 1)
                    if on[1]:
                        count(s - 1, k, 2)
                    if k == 0 and on[4]:
                        copy_b(s - 4, G - 1)
                    if k > 0 and on[3]:
                        copy_b(s - 3, k - 1)
                    if on[1]:
                        count(s - 1, k, 3)
                    if k == 3 and on[3]:
                        head_out(s - 3, 0)
                    if not on[0]:
                        early_parts(s, k)
            steps(act, run)

            heads_back(3)
            deviation(3)
            last_deviation(0)
            last_deviation(1)
            normed_T(3)
            choice_T(3)
            gelu(2)
            last_deviation(2)
            gelu(3)
            last_deviation(3)

        @block.tensor
        def _(pe):
            pe.wait_ge(s_const, 16 * NCONST)
            pe.wait_ge(s_cset, 1)
            with pe.Fori(0, B) as b:
                last = b * NPE
                pe.wait_ge(s_pin, 64 * (b + 1))
                pe.wait_ge(s_pdve, b * NDV)
                vps = psf[:, 4 * 512:4 * 512 + KC * P].rearrange("p (c d) -> p c d", c=KC)
                for c in range(KC):
                    m = P if c < KC - 1 else KR
                    mm = pe.matmul(vps[0:m, c, :], cT[:, c * P:c * P + m], wv, start=True, stop=True)
                mm.then_inc(s_ppe, 1)
                for c in range(4):
                    n = min(512, NK - 512 * c)
                    mm = pe.matmul(ps[:, c, 0:n], wk, cT[:, 512 * c:512 * c + n], start=True, stop=True)
                mm.then_inc(s_ppe, 1)
                pe.wait_ge(s_pdve, b * NDV + 2)
                for c in range(KC):
                    m = P if c < KC - 1 else KR
                    mm = pe.matmul(ps[:, 6, 0:D + 1], cx[0:m, c, 0:D], cx[0:m, c, :],
                                   start=(c == 0), stop=(c == KC - 1))
                mm.then_inc(s_ppe, 1)
                for t in range(QT):
                    mm = pe.transpose(ps[:, 4, t * P:t * P + P], xn[:, t, :], ident[:])
                mm.then_inc(s_ppe, 1)
                pe.wait_ge(s_pdve, b * NDV + 3)
                pe.matmul(ps[:, 7, 0:D], gram[:, 0:D], wk, start=True, stop=True)
                pe.matmul(ps[0:1, 7, D:2 * D], gram[:, D:D + 1], wk, start=True, stop=True)
                pe.matmul(ps[:, 7, 2 * D:2 * D + 1], wk, gram[:, D:D + 1],
                          start=True, stop=True).then_inc(s_ppe, 1)
                pe.wait_ge(s_pact, b * NAC + 3)
                pe.matmul(ps[:, 5, 0:L], wq, xnT, start=True, stop=True).then_inc(s_ppe, 1)
                pe.wait_ge(s_pdve, b * NDV + 4)
                pe.matmul(ps[:, 6, 0:D], wk, t1, start=True, stop=False)
                pe.matmul(ps[:, 6, 0:D], krow[0:1, :], nkrow[0:1, :],
                          start=False, stop=True).then_inc(s_ppe, 1)
                pe.wait_ge(s_pdve, b * NDV + 6)
                pe.matmul(ps[:, 4, 0:L], cov, qf, start=True, stop=True).then_inc(s_ppe, 1)
                pe.wait_ge(s_pdve, b * NDV + 7)
                for t in range(QT):
                    pe.matmul(ps[:, 7, t * 32:t * 32 + H], zq[:, t * P:t * P + P], heads1[:], start=True, stop=True)
                    mm = pe.matmul(ps[:, 7, t * 32 + H:t * 32 + 2 * H], qf[:, t * P:t * P + P], mb,
                                   start=True, stop=True)
                mm.then_inc(s_ppe, 1)
            pe.wait_ge(s_pdve, B * NDV)

            def transposes_a(g, k):
                t = g * G + k
                pe.wait_ge(s_p, t + 1)
                if not isinstance(g, int) or g * G + k >= 1:
                    pe.wait_ge(s_cb, t)
                for c in range(8):
                    mm = pe.transpose(ps[:, 4 + c // 4, c % 4 * P:c % 4 * P + P],
                                      E[k % 2][:, c * P:c * P + P], ident[:])
                mm.then_inc(s_ta, 1)

            def transposes_b(g, k):
                t = g * G + k
                pe.wait_ge(s_ca, t + 1)
                for c in range(8, KC):
                    m = P if c < KC - 1 else KR
                    mm = pe.transpose(ps[0:m, 4 + (c - 8) // 4, c % 4 * P:c % 4 * P + P],
                                      E[k % 2][:, c * P:c * P + m], ident[:])
                mm.then_inc(s_tb, 1)

            def head(g, a):
                pe.wait_ge(s_cb, g * G + 2 * a + 2)
                pe.wait_ge(s_ca, g * G + 2 * a + 2)
                pe.wait_ge(s_vst, 2 * g + a + 1)
                if not isinstance(g, int) or 2 * g + a >= 1:
                    pe.wait_ge(s_ao, 2 * g + a)
                for c in range(KC):
                    m = P if c < KC - 1 else KR
                    mm = pe.matmul(ps[0:DH, 6, 0:L], vst[a][0:m, c, :], PT[a][0:m, c, :],
                                   start=(c == 0), stop=(c == KC - 1))
                mm.then_inc(s_av, 1)

            def scores(s, k):
                if k == 0:
                    pe.wait_ge(s_stk, 96 * (s + 1))
                slot = s % 2 * 2 + k // 2
                for piece in range(2):
                    if not isinstance(s, int) or s * G + k >= 1:
                        pe.wait_ge(s_ev, 2 * G * s + 2 * k - 1 + piece)
                    a, e = (0, CUT) if piece == 0 else (CUT, NK)
                    while a < e:
                        n = min(512, e - a)
                        mm = pe.matmul(psf[:, a:a + n], qst[:, bass.ds(slot, 1), k % 2 * P:k % 2 * P + P]
                                       .rearrange("p a q -> p (a q)"),
                                       kst[:, bass.ds(slot, 1), a:a + n].rearrange("p a k -> p (a k)"),
                                       start=True, stop=True)
                        a += n
                    mm.then_inc(s_sc, 1)

            def heads_by_query(h):
                pe.wait_ge(s_ein[h], 16)
                if h == 2:
                    pe.wait_ge(s_oc, 1)
                if h == 3:
                    pe.wait_ge(s_cb, NT)
                for t in range(QT):
                    mm = pe.transpose(ps_chain(h)[:, t * P:t * P + P], ecT[h][:, t * P:t * P + P], ident[:])
                mm.then_inc(s_hq, 1)

            def heads_back(h):
                pe.wait_ge(s_hn, h + 1)
                for t in range(QT):
                    mm = pe.transpose(ps_chain(h)[:, t * P:t * P + P], ecn[h][:, t * P:t * P + P], ident[:])
                mm.then_inc(s_hb, 1)

            def project(h):
                pe.wait_ge(s_hc, h + 1)
                for t in range(QT):
                    mm = pe.matmul(ps_chain(h)[:, t * P:t * P + P], ecnT[h][:, t * P:t * P + P], wo[:],
                                   start=True, stop=True)
                mm.then_inc(s_wo, 1)

            def normed_T(h):
                pe.wait_ge(s_xn, h + 1)
                for t in range(QT):
                    mm = pe.transpose(ps_chain(h)[:, t * P:t * P + P], xn2[h][:, t * P:t * P + P], ident[:])
                mm.then_inc(s_xt, 1)

            def route(h):
                pe.wait_ge(s_xc, h + 1)
                for t in range(QT):
                    mm = pe.matmul(ps_chain(h)[:, t * NE:t * NE + NE], xnT2[h][:, t * P:t * P + P], wr[:],
                                   start=True, stop=True)
                mm.then_inc(s_rt, 1)

            def choice_T(h):
                pe.wait_ge(s_one, h + 1)
                for t in range(QT):
                    mm = pe.transpose(ps_chain(h)[0:NE, t * P:t * P + P], eone[h][:, t, :], ident[:])
                mm.then_inc(s_ot, 1)

            LATE_MASK = (0, 6)

            def mask(h, e):
                if h + e == 0:
                    pe.wait_ge(s_epb, 1)
                if (h, e) == LATE_MASK:
                    pe.wait_ge(s_sel, NG)
                if e == 0:
                    pe.wait_ge(s_oc, h + 1)
                if h + e > 0:
                    pe.wait_ge(s_xm, h * NE + e)
                pe.matmul(ps_mask, picks_b[:, e * P:e * P + P], oneT_b[h], start=True, stop=True).then_inc(s_mk, 1)

            def up(h, e):
                if e == 0:
                    mask(h, 0)
                    pe.wait_ge(s_ew, 96)
                    if h == 1:
                        pe.wait_ge(s_oc, 3)
                    if h >= 2:
                        pe.wait_ge(s_st2, h - 1)
                    for c in range(NI // P):
                        pe.matmul(ps_up(h, c), b1s[0:NE, c * P:c * P + P], oneT[h],
                                  start=(c % 2 == 0), stop=False)
                if (h, e) == LATE_MASK:
                    mask(h, e)
                pe.wait_ge(s_xm, h * NE + e + 1)
                if e + 1 < NE and (h, e + 1) != LATE_MASK:
                    mask(h, e + 1)
                for c in range(NI // P):
                    mm = pe.matmul(ps_up(h, c), w1_at(e, c), xm[e % 2][:, 0:T],
                                   start=False, stop=(e == NE - 1 and c % 2 == 1))
                mm.then_inc(s_xu, 1)

            def down(h):
                pe.wait_ge(s_gl, NI // P * (h + 1))
                for t in range(QT):
                    for c in range(NI // P):
                        mm = pe.matmul(ps_down(h)[:, t * P:t * P + P], hT[h][:, c, t * P:t * P + P], wfs[:, c, :],
                                       start=(c == 0), stop=(c == NI // P - 1))
                mm.then_inc(s_dn, 1)

            def early_parts(s, k):
                if (s, k) == (NG, 0):
                    heads_by_query(0)
                    heads_by_query(1)
                    heads_back(0)
                    heads_back(1)
                if (s, k) == (NG, 1):
                    project(0)
                    project(1)
                if (s, k) == (NG, 2):
                    normed_T(0)
                    normed_T(1)
                if (s, k) == (NG, 3):
                    for b in range(2):
                        route(b)
                        choice_T(b)
                if s == NG + 1 and k < 3:
                    up(0, 2 * k)
                    up(0, 2 * k + 1)
                if (s, k) == (NG + 1, 0):
                    heads_by_query(2)
                if (s, k) == (NG + 1, 1):
                    heads_back(2)
                if (s, k) == (NG + 1, 2):
                    project(2)
                if (s, k) == (NG + 1, 3):
                    normed_T(2)
                if (s, k) == (NG + 2, 0):
                    route(2)
                    choice_T(2)
                    up(0, 6)
                    up(0, 7)
                if s == NG + 2 and k > 0:
                    up(1, 2 * k - 2)
                    up(1, 2 * k - 1)
                if (s, k) == (NG + 3, 0):
                    up(1, 6)
                if (s, k) == (NG + 3, 1):
                    up(1, 7)
                if (s, k) == (NG + 3, 2):
                    down(0)

            scores(0, 0)

            def run(s, on):
                for k in range(G):
                    if on[0] and k < G - 1:
                        scores(s, k + 1)
                    if on[5] and k == G - 1:
                        scores(s + 1, 0)
                    if k == 0 and on[4]:
                        transposes_b(s - 4, G - 1)
                    if k > 0 and on[3]:
                        transposes_b(s - 3, k - 1)
                    if k == 1 and on[4]:
                        head(s - 4, 1)
                    if k == 3 and on[3]:
                        head(s - 3, 0)
                    if k == 3 and on[2]:
                        pe.wait_ge(s_badr, s - 1)
                        if not on[1]:
                            pe.wait_ge(s_xm, 6)
                        pe.matmul(ps_bad, ones[:], bad[:], start=True, stop=True).then_inc(s_badc, 1)
                    if on[3]:
                        transposes_a(s - 3, k)
                    if not on[0]:
                        early_parts(s, k)
            steps(pe, run)

            up(2, 0)
            down(1)
            up(2, 1)
            heads_by_query(3)
            up(2, 2)
            heads_back(3)
            up(2, 3)
            project(3)
            up(2, 4)
            up(2, 5)
            normed_T(3)
            up(2, 6)
            route(3)
            up(2, 7)
            choice_T(3)
            up(3, 0)
            down(2)
            for e in range(1, NE):
                up(3, e)
            down(3)

        @block.vector
        def _(dve):
            dve.wait_ge(s_const, 16 * NCONST)
            dve.wait_ge(s_cset, 1)

            def parts(src, res, out3):
                dve.tensor_copy(out3[0], src)
                dve.drain()
                dve.tensor_tensor(res, src, out3[0], ALU.subtract)
                dve.drain()
                dve.tensor_copy(out3[1], res)
                dve.drain()
                dve.tensor_tensor(res, res, out3[1], ALU.subtract)
                dve.drain()
                return dve.tensor_copy(out3[2], res)

            with dve.Fori(0, B) as b:
                o = b * NPE
                dve.wait_ge(s_pin, 64 * (b + 1))
                for t in range(QT):
                    dve.bn_stats(stats[:, t, :], xin[:, t, :])
                dve.drain()
                for t in range(QT):
                    ins = dve.bn_aggr(agg[:, t, :], stats[:, t, :])
                ins.then_inc(s_pst, 1)
                dve.wait_ge(s_pact, b * NAC + 1)
                dve.reciprocal(rstd, rstd)
                dve.drain()
                for t in range(QT):
                    ins = dve.tensor_scalar(xn[:, t, :], xin[:, t, :], agg[:, t, 0:1], rstd[:, t:t + 1],
                                            ALU.subtract, ALU.mult)
                ins.then_inc(s_pdve, 1)
                dve.wait_ge(s_ppe, o + 1)
                vps = psf[:, 4 * 512:4 * 512 + KC * P].rearrange("p (c d) -> p c d", c=KC)
                dve.tensor_tensor(V_all[:, 0:KC - 1, bass.ds(b * D, D)], vps[:, 0:KC - 1, :],
                                  bvb.unsqueeze(1).broadcast_to([P, KC - 1, D]), ALU.add)
                dve.tensor_tensor(V_all[0:KR, KC - 1, bass.ds(b * D, D)], vps[0:KR, KC - 1, :],
                                  bvb[0:KR, :], ALU.add).then_inc(s_pdve, 1)
                dve.wait_ge(s_ppe, o + 3)
                dve.tensor_scalar(gram, ps[:, 6, 0:D + 1], 1.0 / NK, None, ALU.mult).then_inc(s_pdve, 1)
                dve.wait_ge(s_ppe, o + 5)
                dve.tensor_copy(t1, ps[:, 7, 0:D])
                dve.tensor_copy(krow[0:1, :], ps[0:1, 7, D:2 * D])
                dve.tensor_scalar(nkrow[0:1, :], ps[0:1, 7, D:2 * D], -1.0, None, ALU.mult)
                dve.tensor_tensor(kb, ps[:, 7, 2 * D:2 * D + 1], bkc[:], ALU.add)
                dve.drain()
                dve.tensor_scalar(mb, heads1[:], kb, None, ALU.mult).then_inc(s_pdve, 1)
                dve.wait_ge(s_ppe, o + 6)
                dve.wait_ge(s_pout, b * 192)
                dve.tensor_scalar(qf, ps[:, 5, 0:L], bqc[:], QSCALE, ALU.add, ALU.mult)
                dve.drain()
                parts(qf, qres, qp).then_inc(s_pdve, 1)
                dve.wait_ge(s_ppe, o + 7)
                dve.tensor_tensor(cov, ps[:, 6, 0:D], blocks, ALU.mult).then_inc(s_pdve, 1)
                dve.wait_ge(s_ppe, o + 8)
                dve.tensor_tensor(zq, ps[:, 4, 0:L], qf, ALU.mult).then_inc(s_pdve, 1)
                dve.wait_ge(s_ppe, o + 9)
                st = ps[:, 7, 0:QT * 32].rearrange("p (t s) -> p t s", t=QT)
                dve.tensor_scalar(var, st[:, :, 0:H], 0.0, None, ALU.max).then_inc(s_pdve, 1)
                dve.wait_ge(s_pact, b * NAC + 4)
                c = bass.ds(b * H * QT, H * QT)
                by_t = lambda arr: arr[:, c].rearrange("p (h t) -> p t h", t=QT)
                dve.tensor_scalar(by_t(unit), sig, SLOPE, None, ALU.mult)
                dve.tensor_scalar(by_t(nthr), sig, -SHIFT, None, ALU.mult)
                dve.scalar_tensor_tensor(by_t(shift), sig, SHIFT, st[:, :, H:2 * H],
                                         ALU.mult, ALU.subtract).then_inc(s_pdve, 1)
                parts(kf, kres, kp).then_inc(s_pdve, 1)

            def select(g, k):
                t = g * G + k
                dve.wait_ge(s_cnt[3], t + 1)
                if k % 2 == 0:
                    dve.tensor_scalar(trial[:, k:k + 2], nthr[:, col(g * G + k, 2)], -1.0, None, ALU.mult)
                    dve.drain()
                sc = S_at(g % RING, k)
                dve.scalar_tensor_tensor(y[:], sc, trial[:, k:k + 1], sc, ALU.is_le, ALU.mult)
                dve.drain()
                for i in range(NSEG):
                    e = (i + 1) * SEG if i < NSEG - 1 else NK
                    dve.max(cand[:, k, 8 * i:8 * i + 8], y[:, i * SEG:e])
                dve.drain()

            def settle(g):
                c = col(g * G, G)
                n = NV - 1
                for i in range(3):
                    src = cand if i == 0 else cand2
                    for k in range(G):
                        dve.max(top[:, k, 8 * i:8 * i + 8], src[:, k, :])
                    dve.drain()
                    if i < 2:
                        for k in range(G):
                            dve.match_replace(cand2[:, k, :], top[:, k, 8 * i:8 * i + 8], src[:, k, :], 0.0)
                        dve.drain()
                dve.tensor_scalar(rank[:], sgn[:, c], -0.5, TOPK - NK / 2 + 0.25, ALU.mult, ALU.add)
                dve.tensor_reduce(seg8[:], cand[:, :, 7:8 * NSEG:8], AX.X, ALU.max)
                dve.drain()
                dve.tensor_scalar(rank[:], rank[:], 2.0 ** 23, -2.0 ** 23, ALU.add, ALU.add)
                dve.drain()
                dve.tensor_tensor(hit[:], ranks[:].unsqueeze(1).broadcast_to([P, G, n]),
                                  rank[:].unsqueeze(2).broadcast_to([P, G, n]), ALU.is_equal)
                dve.drain()
                dve.tensor_tensor(pick[:], hit[:], top[:, :, 0:n], ALU.mult)
                dve.drain()
                dve.tensor_reduce(thr[:, c], pick[:], AX.X, ALU.add)
                dve.drain()
                dve.tensor_tensor(pick[:], hit[:], top[:, :, 1:n + 1], ALU.mult)
                dve.drain()
                dve.tensor_reduce(nxt[:], pick[:], AX.X, ALU.add)
                dve.drain()
                dve.tensor_tensor(bad[:], seg8[:], thr[:, c], ALU.is_lt)
                dve.tensor_tensor(bad2[:], top[:, :, 1], trial[:], ALU.is_lt)
                dve.drain()
                dve.tensor_scalar(seg8[:], thr[:, c], 0.0, None, ALU.is_gt)
                dve.tensor_tensor(bad[:], bad[:], bad2[:], ALU.mult)
                dve.drain()
                dve.tensor_tensor(bad[:], bad[:], seg8[:], ALU.mult)
                dve.tensor_tensor(nxt[:], nxt[:], thr[:, c], ALU.is_equal)
                dve.drain()
                dve.tensor_scalar(bad[:], bad[:], -LOST, LOST, ALU.mult, ALU.add)
                dve.drain()
                dve.tensor_tensor(bad[:], bad[:], nxt[:], ALU.add).then_inc(s_badr, 1)

            def bisect(g, k):
                t = g * G + k
                sc = S_at(g % RING, k)
                top_s = nmax[:, col(t)]
                dve.tensor_scalar(y[:], sc, 1.0, None, ALU.mult, ALU.min, accum_out=lo[:])
                dve.tensor_scalar(mid[:], top_s, -1.0, None, ALU.mult)
                dve.drain()
                dve.tensor_tensor(hi[:], mid[:], lo[:], ALU.subtract)
                dve.tensor_tensor(w0[:], mid[:], top_s, ALU.max)
                dve.drain()
                dve.tensor_tensor(hi[:], hi[:], mid[:], ALU.add)
                dve.drain()
                dve.scalar_tensor_tensor(hi[:], hi[:], 1.0 / BIG, w0[:], ALU.add, ALU.add)
                dve.drain()
                with dve.Fori(0, BISECT):
                    dve.tensor_tensor(mid[:], lo[:], hi[:], ALU.add)
                    dve.drain()
                    dve.tensor_scalar(mid[:], mid[:], 0.5, None, ALU.mult)
                    dve.drain()
                    dve.tensor_scalar(y[:], sc, mid[:], None, ALU.is_ge, ALU.add, accum_out=cnt[:])
                    dve.drain()
                    dve.tensor_scalar(keep[:], cnt[:], TOPK - 0.5, None, ALU.is_ge)
                    dve.drain()
                    dve.tensor_scalar(w0[:], keep[:], 1.0, BIG, ALU.subtract, ALU.mult)
                    dve.tensor_tensor(w1[:], keep[:], mid[:], ALU.mult)
                    dve.drain()
                    dve.tensor_tensor(w0[:], w0[:], w1[:], ALU.add)
                    dve.tensor_tensor(w2[:], mid[:], w1[:], ALU.subtract)
                    dve.drain()
                    dve.tensor_tensor(lo[:], lo[:], w0[:], ALU.max)
                    dve.scalar_tensor_tensor(w2[:], keep[:], BIG, w2[:], ALU.mult, ALU.add)
                    dve.drain()
                    dve.tensor_tensor(hi[:], hi[:], w2[:], ALU.min)
                    dve.drain()

            def break_tie(g, k, above, under):
                t = g * G + k
                sc = S_at(g % RING, k)
                dve.tensor_scalar(y[:], sc, hi[:], None, above, ALU.add, accum_out=cnt[:])
                dve.drain()
                dve.tensor_scalar(keep[:], cnt[:], -1.0, float(TOPK), ALU.mult, ALU.add)
                dve.tensor_scalar(y[:], sc, lo[:], 0.5, ALU.is_ge, ALU.mult)
                dve.drain()
                dve.scalar_tensor_tensor(y[:], sc, hi[:], y[:], under, ALU.mult)
                dve.drain()
                dve.tensor_tensor_scan(y[:], y[:], y[:], 0.0, ALU.add, ALU.add)
                dve.drain()
                dve.tensor_scalar(y[:], y[:], keep[:], -BIG, ALU.is_gt, ALU.mult)
                dve.drain()
                dve.scalar_tensor_tensor(y[:], sc, hi[:], y[:], under, ALU.mult)
                dve.drain()
                dve.tensor_tensor(sc, sc, y[:], ALU.add)
                dve.tensor_copy(thr[:, col(t)], lo[:])
                dve.drain()

            def by_tile(a):
                return a.rearrange("p (n d) -> p n d", d=D)

            def divide(h):
                a = h * H * QT
                dve.reciprocal(rz[h].rearrange("p (t a) -> p t a", t=QT),
                               Z[:, a:a + H * QT].rearrange("p (a t) -> p t a", t=QT))
                dve.drain()
                dve.wait_ge(s_hq, h + 1)
                dve.tensor_tensor(ecn[h].rearrange("p (a d) -> p a d", d=DH),
                                  ps_chain(h).rearrange("p (a d) -> p a d", d=DH),
                                  rz[h].unsqueeze(2).broadcast_to([P, QT * H, DH]), ALU.mult).then_inc(s_hn, 1)

            def statistics(src, h):
                for t in range(QT):
                    dve.bn_stats(est[h][:, t, :], src[h][:, t * P:t * P + P])
                dve.drain()
                for t in range(QT):
                    ins = dve.bn_aggr(eag[h][:, t, :], est[h][:, t, :])
                return ins

            def residual(h):
                dve.wait_ge(s_exb, h + 1)
                dve.wait_ge(s_wo, h + 1)
                dve.tensor_tensor(x1[h], ps_chain(h), xb[h], ALU.add)
                dve.drain()
                statistics(x1, h).then_inc(s_st1, 1)

            def norm(h):
                dve.wait_ge(s_sd1, h + 1)
                dve.reciprocal(estd[h], estd[h])
                dve.drain()
                for t in range(QT):
                    q = slice(t * P, t * P + P)
                    ins = dve.tensor_scalar(xn2[h][:, q], x1[h][:, q], eag[h][:, t, 0:1], estd[h][:, t:t + 1],
                                            ALU.subtract, ALU.mult)
                ins.then_inc(s_xn, 1)

            def choose(h):
                logits = ps_chain(h)[:, 0:QT * NE].rearrange("p (t e) -> p t e", e=NE)
                top1 = emx[h].unsqueeze(2).broadcast_to([P, QT, NE])
                dve.wait_ge(s_rt, h + 1)
                dve.tensor_reduce(emx[h], logits, AX.X, ALU.max)
                dve.drain()
                dve.tensor_tensor(elog[h], logits, top1, ALU.is_equal)
                dve.drain()
                dve.tensor_tensor(elog[h], elog[h], firsts[:].unsqueeze(1).broadcast_to([P, QT, NE]), ALU.mult)
                dve.drain()
                dve.tensor_reduce(emx[h], elog[h], AX.X, ALU.max)
                dve.drain()
                dve.tensor_tensor(eone[h], elog[h], top1, ALU.is_equal).then_inc(s_one, 1)

            def tokens(h, e):
                if h * NE + e >= 2:
                    dve.wait_ge(s_xu, h * NE + e - 1)
                dve.wait_ge(s_mk, h * NE + e + 1)
                dve.wait_ge(s_xc, h + 1)
                dve.tensor_tensor(xm[e % 2][:, 0:T], ps_mask, xnT2[h], ALU.mult).then_inc(s_xm, 1)

            def add_up(h):
                dve.wait_ge(s_ads, 2 * h + 2)
                dve.wait_ge(s_dn, h + 1)
                dve.tensor_tensor(ey[h], ps_down(h), xnb[h], ALU.add)
                dve.drain()
                statistics(ey, h).then_inc(s_st2, 1)

            def finish(h):
                dve.wait_ge(s_sd2, h + 1)
                dve.reciprocal(estd[h], estd[h])
                dve.drain()
                for t in range(QT):
                    q = slice(t * P, t * P + P)
                    dve.tensor_scalar(ey[h][:, q], ey[h][:, q], eag[h][:, t, 0:1], estd[h][:, t:t + 1],
                                      ALU.subtract, ALU.mult)
                dve.drain()
                dve.tensor_tensor(by_tile(ey[h]), by_tile(ey[h]), gab[:].unsqueeze(1).broadcast_to([P, QT, D]), ALU.mult)
                dve.drain()
                dve.tensor_tensor(ey[h], ey[h], x1b[h], ALU.add).then_inc(s_fin, 1)

            def early_parts(s, k):
                if (s, k) == (NG, 0):
                    divide(0)
                    divide(1)
                if (s, k) == (NG, 1):
                    residual(0)
                    residual(1)
                if (s, k) == (NG, 2):
                    norm(0)
                    norm(1)
                if (s, k) == (NG, 3):
                    choose(0)
                    choose(1)
                if s == NG + 1 and k < 3:
                    tokens(0, 2 * k)
                    tokens(0, 2 * k + 1)
                if (s, k) == (NG + 1, 1):
                    divide(2)
                if (s, k) == (NG + 1, 3):
                    residual(2)
                    norm(2)
                if (s, k) == (NG + 2, 0):
                    choose(2)
                    tokens(0, 6)
                    tokens(0, 7)
                if s == NG + 2 and k > 0:
                    tokens(1, 2 * k - 2)
                    tokens(1, 2 * k - 1)
                if (s, k) == (NG + 3, 0):
                    tokens(1, 6)
                if (s, k) == (NG + 3, 1):
                    tokens(1, 7)
                if (s, k) == (NG + 3, 2):
                    add_up(0)

            def run(s, on):
                for k in range(G):
                    if on[0]:
                        t = s * G + k
                        for piece in range(2):
                            a, n = (0, CUT) if piece == 0 else (CUT, NK - CUT)
                            dve.wait_ge(s_sc, 2 * t + piece + 1)
                            dve.tensor_scalar(S_at(s % RING, k, a, n), psf[:, a:a + n], shift[:, col(t)], None,
                                              ALU.add, ALU.max, accum_out=mx[:, k, piece:piece + 1]
                                              ).then_inc(s_ev, 1)
                    if on[2]:
                        select(s - 2, k)
                    if k == 3 and on[2]:
                        settle(s - 2)
                    if on[3]:
                        g = s - 3
                        dve.wait_ge(s_exp, g * G + k + 1)
                        e = E[k % 2][:]
                        dve.scalar_tensor_tensor(e, S_at(g % RING, k), thr[:, col(g * G + k)], e,
                                                 ALU.is_ge, ALU.mult,
                                                 accum_out=Z[:, col(g * G + k)]).then_inc(s_p, 1)
                    if not on[0]:
                        early_parts(s, k)
                if on[0]:
                    dve.drain()
                    dve.tensor_tensor(nmax[:, col(s * G, G)], mx[:, :, 0], mx[:, :, 1], ALU.max)
                    dve.drain()
                    dve.tensor_scalar(nmax[:, col(s * G, G)], nmax[:, col(s * G, G)], -1.0, None, ALU.mult)
                if on[2]:
                    g = s - 2
                    dve.wait_ge(s_badc, g + 1)
                    dve.tensor_copy(badi[:, 0:G], ps_bad)
                    dve.tensor_reduce(badf[:], ps_bad, AX.X, ALU.add)
                    dve.drain()
                    dve.tensor_copy(badi[:, G:G + 1], badf[:])
                    dve.drain()
                    rows = dve.value_load(badi[0:1, G:G + 1], min_val=0, max_val=G * MOST)
                    with dve.If(rows > 0):
                        with dve.Fori(0, G) as k:
                            mine = dve.value_load(badi[0:1, bass.ds(k, 1)], min_val=0, max_val=MOST)
                            with dve.If(mine >= int(LOST)):
                                bisect(g, k)
                                break_tie(g, k, ALU.is_ge, ALU.is_lt)
                            with dve.Else():
                                with dve.If(mine > 0):
                                    dve.tensor_copy(lo[:], thr[:, col(g * G + k)])
                                    dve.tensor_copy(hi[:], thr[:, col(g * G + k)])
                                    dve.drain()
                                    break_tie(g, k, ALU.is_gt, ALU.is_le)
                    dve.drain().then_inc(s_sel, 1)
            steps(dve, run)

            tokens(2, 0)
            tokens(2, 1)
            add_up(1)
            tokens(2, 2)
            divide(3)
            tokens(2, 3)
            tokens(2, 4)
            residual(3)
            tokens(2, 5)
            norm(3)
            tokens(2, 6)
            tokens(2, 7)
            choose(3)
            tokens(3, 0)
            tokens(3, 1)
            add_up(2)
            tokens(3, 2)
            finish(0)
            tokens(3, 3)
            finish(1)
            tokens(3, 4)
            finish(2)
            for e in range(5, NE):
                tokens(3, e)
            add_up(3)
            finish(3)


def kernel(**inputs):
    import concourse.bacc as bacc
    from concourse.bass_utils import run_bass_kernel_spmd as run

    nc = bacc.Bacc("TRN2", target_bir_lowering=False, num_devices=1)
    a = {k: np.asarray(v) for k, v in inputs.items()}
    head_of = np.arange(P) // DH
    arrays = {
        "x": a["x"].reshape(B * L, D),
        "ctx": a["ctx_1024"].reshape(B * NK, D),
        "ctxT": a["ctx_1024"].transpose(0, 2, 1).reshape(B * D, NK),
        "WqT": a["L0_xattn_Wq"].T, "bq": a["L0_xattn_bq"],
        "WkT": a["L0_xattn_Wk"].T, "bk": a["L0_xattn_bk"],
        "WvT": a["L0_xattn_Wv"].T, "bv": a["L0_xattn_bv"],
        "WoT": a["L0_xattn_Wo"].T, "bo": a["L0_xattn_bo"],
        "WrT": a["L0_ffn_Wr"].T, "W1": a["L0_ffn_W1"], "b1": a["L0_ffn_b1"],
        "Wf": a["L0_ffn_Wo"], "bf": a["L0_ffn_bo"],
        "gamma": a["L0_ffn_gamma"], "beta": a["L0_ffn_beta"],
        "ident": np.eye(P, dtype=np.float32),
        "blocks": (head_of[:, None] == head_of[None, :]).astype(np.float32),
        "heads": (head_of[:, None] == np.arange(H)[None, :]).astype(np.float32),
        "ranks": np.tile(np.arange(1, NV, dtype=np.float32), (P, 1)),
        "firsts": np.tile(np.arange(NE, 0, -1, dtype=np.float32), (P, 1)),
        "picks": np.repeat(np.eye(NE, dtype=np.float32), P, axis=1),
    }
    args = []
    for name in arrays:
        arrays[name] = np.ascontiguousarray(arrays[name])
        args.append(nc.dram_tensor(f"in_{name}", arrays[name].shape, F32, kind="ExternalInput").ap())
    args.append(nc.dram_tensor("out", (B * L, D), F32, kind="ExternalOutput").ap())
    build(nc, *args)
    r = run(nc, [{f"in_{k}": v for k, v in arrays.items()}], core_ids=[0])
    return r.results[0]["out"].reshape(B, L, D)
```

```python
from contextlib import ExitStack

import numpy as np
import concourse.bass as bass
from concourse import mybir

F32 = mybir.dt.float32
BF16 = mybir.dt.bfloat16
I32 = mybir.dt.int32
ALU = mybir.AluOpType
ACT = mybir.ActivationFunctionType
AX = mybir.AxisListType

P = 128
B, L, D = 4, 256, 128
NK = 1601
H, DH = 16, 8
TOPK = NK // 2
NI, NE = 512, 8
KC = 13
KR = NK - (KC - 1) * P
QT = L // P
G = 2 * QT
NG = B * H * QT // G
NT = B * H * QT
RING = 4
CUT = 1024
PART = DH * 3

NSEG = 8
SEG = NK // NSEG
NV = 24
AIM = 8
LAST_AIM = 9
LEAN = 0.2
SHIFT = 1.0
SLOPE = 1.0 / (2 * NK * 0.4)
STIFF = 600.0
BISECT = 48
BIG = 1e30
LOST = 1024.0
MOST = P * (int(LOST) + 1)
QSCALE = float(1.0 / np.sqrt(DH))


def build(nc, x, ctx, ctxT, WqT, bq, WkT, bk, WvT, bv, WoT, bo, WrT, W1, b1, Wf, bf, gamma, beta,
          ident_in, blocks_in, heads_in, ranks_in, firsts_in, picks_in, out):
    with ExitStack() as es:
        def sb(name, shape, dt=F32):
            return es.enter_context(nc.sbuf_tensor(name, shape, dt))

        def sem(name):
            return es.enter_context(nc.semaphore(name))

        k_parts = nc.dram_tensor("k_parts", [B * H * PART, NK], BF16).ap()
        q_parts = [nc.dram_tensor(f"q_parts{g}", [B * H * PART, L], BF16).ap() for g in range(3)]

        S = sb("S", [P, RING * G * NK])
        y = [sb(f"y{i}", [P, NK]) for i in range(2)]
        E = [sb(f"E{i}", [P, NK]) for i in range(2)]
        signs = sb("signs", [P, G, NK], mybir.dt.int8)
        kst_flat = sb("kst", [P, 4 * NK], BF16)
        kst = kst_flat[:].rearrange("p (a k) -> p a k", a=4)
        qst = sb("qst", [P, 4, L], BF16)
        PT = [sb(f"PT{i}", [P, KC, P]) for i in range(2)]
        V_all = sb("V_all", [P, KC, B * D])
        heads_q = sb("heads_q", [P, NG * G * DH])
        cand = sb("cand", [P, G, NSEG * 8])
        cand2 = sb("cand2", [P, G, NSEG * 8])
        top = sb("top", [P, G, NV])
        hit = sb("hit", [P, G, NV - 1])
        pick = sb("pick", [P, 2 * G, NV - 1])
        sums = sb("sums", [P, 2 * G])
        thr4, nxt = sums[:, 0:G], sums[:, G:2 * G]
        found = sb("found", [P, G])
        c_one4 = sb("c_one4", [P, G])
        rank = sb("rank", [P, G])
        seg8 = sb("seg8", [P, G])
        bad = sb("bad", [P, G])
        bad2 = sb("bad2", [P, G])
        badf = sb("badf", [1, 1])
        badi = sb("badi", [1, G + 1], I32)
        mx = sb("mx", [P, G, 2])
        shift = sb("shift", [P, NT])
        unit = sb("unit", [P, NT])
        trial = sb("trial", [P, NT])
        thr = sb("thr", [P, NT])
        nmax = sb("nmax", [P, NT])
        sgn = sb("sgn", [P, NT])
        fprev = sb("fprev", [P, NT])
        step_c = sb("step_c", [P, NT])
        ratio = sb("ratio", [P, NT])
        Z = sb("Z", [P, NT])
        c_aim = sb("c_aim", [P, G // 2])
        c_one = sb("c_one", [P, G // 2])
        c_stiff = sb("c_stiff", [P, G // 2])
        c_neg = sb("c_neg", [P, G // 2])
        g_wait, a_wait = sb("g_wait", [P, G // 2]), sb("a_wait", [P, 2])
        g_f = sb("g_f", [P, G // 2])
        g_df = sb("g_df", [P, G // 2])
        g_num = sb("g_num", [P, G // 2])
        g_old = sb("g_old", [P, G // 2])
        g_den = sb("g_den", [P, G // 2])
        g_r = sb("g_r", [P, G // 2])
        g_e = sb("g_e", [P, G // 2])
        g_d = sb("g_d", [P, G // 2])
        lo, hi, mid, cnt, keep, w0, w1, w2 = (sb(n, [P, 1]) for n in ("lo", "hi", "mid", "cnt", "keep", "w0", "w1", "w2"))
        ident = sb("ident", [P, P])
        heads1 = sb("heads1", [P, H])
        ranks = sb("ranks", [P, NV - 1])
        firsts = sb("firsts", [P, NE])
        ones = sb("ones", [P, 1])
        wo = sb("wo", [P, D])
        wr = sb("wr", [P, NE])
        bqc, bkc = sb("bqc", [P, 1]), sb("bkc", [P, 1])
        bob, bfb, gab, beb = (sb(n, [P, D]) for n in ("bob", "bfb", "gab", "beb"))
        eps5, eps12 = sb("eps5", [P, 1]), sb("eps12", [P, 1])

        ps = es.enter_context(nc.psum_tensor("ps", [P, 8, 512], F32))
        psf = ps[:].rearrange("p a b -> p (a b)")

        used = [0]

        def carve(n, dt=F32):
            a = S[:, used[0]:used[0] + n]
            used[0] += n
            if dt == BF16:
                a = a.bitcast(BF16)
            return a

        wq, wk, wv, bvb, blocks = (carve(D) for _ in range(5))
        cT = [carve(NK) for _ in range(2)]
        cx = [carve(KC * (D + 1)).rearrange("p (c d) -> p c d", c=KC) for _ in range(2)]
        xin = [carve(QT * D).rearrange("p (t d) -> p t d", t=QT) for _ in range(2)]
        kf = [carve(NK) for _ in range(2)]
        kp = [[carve(NK // 2 + 1, BF16)[:, 0:NK] for _ in range(3)] for _ in range(2)]
        qf = [carve(L) for _ in range(2)]
        qp = [[carve(L // 2, BF16) for _ in range(3)] for _ in range(2)]
        kres = carve(NK)
        qres = carve(L)
        xn = carve(QT * D).rearrange("p (t d) -> p t d", t=QT)
        xnT = carve(L)
        gram = carve(D + 1)
        t1 = carve(D)
        krow = carve(D)
        nkrow = carve(D)
        cov = carve(D)
        mb = carve(H)
        kb = carve(1)
        zq = carve(L)
        var = carve(QT * H).rearrange("p (t h) -> p t h", t=QT)
        mean = carve(QT * H).rearrange("p (t h) -> p t h", t=QT)
        sig = carve(QT * H).rearrange("p (t h) -> p t h", t=QT)
        stats = carve(QT * 6).rearrange("p (t s) -> p t s", t=QT)
        agg = carve(QT * 2).rearrange("p (t s) -> p t s", t=QT)
        rstd = carve(QT)
        assert used[0] <= RING * G * NK

        T = QT * P

        def carve_from(slot):
            used[0] = slot * G * NK

        def each(n, m=B):
            return [carve(n) for _ in range(m)]

        def tiles(arr):
            return [a.rearrange("p (t d) -> p t d", t=QT) for a in arr]

        carve_from(0)
        xb = each(T)
        ecn, ecnT, x1, xn2, xnT2 = (each(T, 3) for _ in range(5))
        xm = each(T, 2)
        rz, estd, emx = each(QT * H), each(QT), each(QT)
        est, eag, elog, eone = (tiles(each(QT * n)) for n in (6, 2, NE, NE))
        b1s = carve(NI)
        assert used[0] <= G * NK
        carve_from(1)
        for a in (ecn, ecnT, x1, xn2, xnT2):
            a += each(T, 1)
        wfs = carve(NI // P * D).rearrange("p (c d) -> p c d", c=NI // P)
        hT = [carve(NI * QT).rearrange("p (c q) -> p c q", c=NI // P) for _ in range(2)]
        assert used[0] <= 2 * G * NK
        carve_from(2)
        hT += [carve(NI * QT).rearrange("p (c q) -> p c q", c=NI // P) for _ in range(2)]
        xnb, x1b, ey = (each(T) for _ in range(3))
        assert used[0] <= 3 * G * NK
        assert NE + (NE + 2) // 3 < KC and NI == 4 * P and B == 4

        def w1_at(e, c):
            return (V_all[:, e, c * P:c * P + P] if c < 3 else
                    V_all[:, NE + e // 3, e % 3 * P:e % 3 * P + P])

        kfree = kst_flat[:].bitcast(F32)
        picks = kfree[0:NE, 0:NE * P]
        oneT = [kfree[0:NE, NE * P + b * T:NE * P + b * T + T] for b in range(B)]
        used_b = 2 * (NE * P + B * T)
        picks_b = kst_flat[0:NE, used_b:used_b + NE * P]
        used_b += NE * P
        oneT_b = [kst_flat[0:NE, used_b + b * T:used_b + b * T + T] for b in range(B)]
        assert used_b + B * T <= 4 * NK

        s_const = sem("s_const")
        s_cset1 = sem("s_cset1")
        s_cset = sem("s_cset")
        s_w = sem("s_w")
        s_pin = [sem(f"s_pin{i}") for i in range(2)]
        s_va = sem("s_va")
        s_vb = sem("s_vb")
        s_vac = sem("s_vac")
        s_vbc = sem("s_vbc")
        s_k = sem("s_k")
        s_kc = sem("s_kc")
        s_kr = sem("s_kr")
        s_k1 = sem("s_k1")
        s_kp = sem("s_kp")
        s_pst = sem("s_pst")
        s_psd = sem("s_psd")
        s_pxn = sem("s_pxn")
        s_pxt = sem("s_pxt")
        s_pxc = sem("s_pxc")
        s_q = sem("s_q")
        s_qp = sem("s_qp")
        s_m = sem("s_m")
        s_mc = sem("s_mc")
        s_mk2 = sem("s_mk2")
        s_mk2c = sem("s_mk2c")
        s_cv = sem("s_cv")
        s_cvc = sem("s_cvc")
        s_z = sem("s_z")
        s_zc = sem("s_zc")
        s_vm = sem("s_vm")
        s_vmc = sem("s_vmc")
        s_sg = sem("s_sg")
        s_st0 = sem("s_st0")
        s_pout = [sem(f"s_pout{i}") for i in range(2)]
        s_stk = sem("s_stk")
        s_sc = sem("s_sc")
        s_ev = sem("s_ev")
        s_cnt = [sem(f"s_cnt{i}") for i in range(4)]
        s_thr = [sem(f"s_thr{i}") for i in range(4)]
        s_top = sem("s_top")
        s_badr = sem("s_badr")
        s_badc = sem("s_badc")
        s_bad = sem("s_bad")
        s_sel = sem("s_sel")
        s_exp = sem("s_exp")
        s_p = sem("s_p")
        s_t = sem("s_t")
        s_cb = sem("s_cb")
        s_av = sem("s_av")
        s_ao = sem("s_ao")
        s_ex = sem("s_ex")
        s_ew = sem("s_ew")
        s_epk = sem("s_epk")
        s_epb = sem("s_epb")
        s_exb = sem("s_exb")
        s_hn = sem("s_hn")
        s_hb = sem("s_hb")
        s_hc = sem("s_hc")
        s_wo = sem("s_wo")
        s_x1 = sem("s_x1")
        s_st1 = sem("s_st1")
        s_sd1 = sem("s_sd1")
        s_xn = sem("s_xn")
        s_xt = sem("s_xt")
        s_xc = sem("s_xc")
        s_rt = sem("s_rt")
        s_one = sem("s_one")
        s_ot = sem("s_ot")
        s_oc = sem("s_oc")
        s_mk = sem("s_mk")
        s_xm = sem("s_xm")
        s_xu = sem("s_xu")
        s_gl = sem("s_gl")
        s_dn = sem("s_dn")
        s_ads = sem("s_ads")
        s_st2 = sem("s_st2")
        s_sd2 = sem("s_sd2")
        s_fin = sem("s_fin")
        s_out = sem("s_out")

        NW = 6
        NCONST = 11

        ps_heads = ps[:, 3, P:P + G * DH]
        ps_bad = ps[0:1, 3, 2 * P:2 * P + G]

        CHAIN = [0, 1, 2, 6]
        UP = [0, 0, 4, 0]

        def ps_chain(b):
            return ps[:, CHAIN[b], 0:T]

        def ps_up(b, c):
            return ps[:, UP[b] + c // 2, c % 2 * T:c % 2 * T + T]

        ps_down = ps[:, 7, 0:T]
        ps_mask = ps[:, 2, 0:T]

        def S_at(slot, k, a=0, n=NK):
            return S[:, bass.ds((slot * G + k) * NK + a, n)]

        def col(t, n=1):
            return bass.ds(t, n)

        def steps(eng, run):
            def stages(s):
                return [0 <= s - i < NG for i in range(5)] + [s + 1 < NG]
            for s in range(4):
                run(s, stages(s))
            with eng.Fori(4, NG - 1) as s:
                run(s, [True] * 6)
            for s in range(NG - 1, NG + 4):
                run(s, stages(s))

        block = es.enter_context(nc.Block())

        @block.sync
        def _(sp):
            def column(vec):
                return vec.rearrange("(p a) -> p a", a=1)

            full = (KC - 1) * P

            def stacked(s):
                if not isinstance(s, int) or s >= 2:
                    sp.wait_ge(s_sc, 2 * G * (s - 1))
                if not isinstance(s, int) or s >= 1:
                    sp.wait_ge(s_stk, 96 * s)
                slot = s % 2 * 2
                for g in range(3):
                    sp.dma_start(kst[32 * g:32 * g + PART, bass.ds(slot, 2), :],
                                 k_parts[bass.ds(s * 2 * PART, 2 * PART), :]
                                 .rearrange("(a r) k -> r a k", a=2)).then_inc(s_stk, 16)
                    sp.dma_start(qst[32 * g:32 * g + PART, bass.ds(slot, 2), :],
                                 q_parts[g][bass.ds(s * 2 * PART, 2 * PART), :]
                                 .rearrange("(a r) k -> r a k", a=2)).then_inc(s_stk, 16)

            def inputs(b):
                if b >= 2:
                    sp.wait_ge(s_m, b - 1)
                    sp.wait_ge(s_pxn, b - 1)
                i = b % 2
                sp.dma_start(cT[i], ctxT[b * D:b * D + D, :]).then_inc(s_pin[i], 16)
                sp.dma_start(xin[i], x[b * L:b * L + L, :].rearrange("(t p) d -> p t d", p=P)).then_inc(s_pin[i], 16)
                sp.dma_start(cx[i][:, 0:KC - 1, 0:D],
                             ctx[b * NK:b * NK + full, :].rearrange("(c p) d -> p c d", p=P)).then_inc(s_pin[i], 16)
                sp.dma_start(cx[i][0:KR, KC - 1, 0:D], ctx[b * NK + full:(b + 1) * NK, :]).then_inc(s_pin[i], 16)

            sp.dma_start(wv, WvT).then_inc(s_w, 16)
            sp.dma_start(wk, WkT).then_inc(s_w, 16)
            inputs(0)
            for dst, src in ((ident[:], ident_in), (wq, WqT), (bkc[:], column(bk)),
                             (bvb, bv.rearrange("(a d) -> a d", a=1).broadcast_to([P, D]))):
                sp.dma_start(dst, src).then_inc(s_w, 16)
            for dst, src in ((bqc[:], column(bq)), (blocks, blocks_in), (heads1[:], heads_in)):
                sp.dma_start(dst, src).then_inc(s_const, 16)
            inputs(1)
            for dst, src in ((ranks, ranks_in), (firsts, firsts_in), (wo, WoT), (wr, WrT)):
                sp.dma_start(dst[:, :], src).then_inc(s_const, 16)
            for dst, src in ((bob, bo), (bfb, bf), (gab, gamma), (beb, beta)):
                sp.dma_start(dst[:, :], src.rearrange("(a d) -> a d", a=1).broadcast_to([P, D])).then_inc(s_const, 16)
            for b in range(B):
                rows = slice(b * H * PART, (b + 1) * H * PART)
                if b >= 2:
                    sp.wait_ge(s_pout[b % 2], 12 * 16)
                if b == 2:
                    sp.wait_ge(s_cset, 1)
                    stacked(0)
                sp.wait_ge(s_qp, b + 1)
                for g in range(3):
                    dst = q_parts[g][rows, :].rearrange("(r j) q -> r j q", j=3)
                    for j in range(3):
                        sp.dma_start(dst[:, j, :], qp[b % 2][g]).then_inc(s_pout[b % 2], 16)
                if b + 2 < B:
                    inputs(b + 2)
                sp.wait_ge(s_kp, b + 1)
                dst = k_parts[rows, :].rearrange("(r j) k -> r j k", j=3)
                for j in range(3):
                    sp.dma_start(dst[:, j, :], kp[b % 2][j]).then_inc(s_pout[b % 2], 16)
            for i in range(2):
                sp.wait_ge(s_pout[i], 12 * 16 * (B // 2))

            def epilogue_loads(s):
                if s == NG - 1:
                    sp.wait_ge(s_av, NT // B * (B - 1))
                    sp.dma_start(V_all[:, 0:NE, 0:3 * P], W1[:, :, 0:3 * P].rearrange("e d n -> d e n")).then_inc(s_ew, 16)
                    for e in range(0, NE, 3):
                        n = min(3, NE - e)
                        sp.dma_start(V_all[:, NE + e // 3, 0:n * P].rearrange("p (e n) -> p e n", e=n),
                                     W1[e:e + n, :, 3 * P:].rearrange("e d n -> d e n")).then_inc(s_ew, 16)
                if s == NG:
                    sp.wait_ge(s_p, G * (NG - RING + 1))
                    for b in range(B):
                        sp.dma_start(xb[b].rearrange("p (n d) -> p n d", n=QT),
                                     x[b * T:b * T + T, :].rearrange("(n p) d -> p n d", p=P)).then_inc(s_ex, 16)
                    sp.dma_start(b1s[0:NE, :], b1).then_inc(s_ew, 16)
                    sp.wait_ge(s_sc, 2 * NT)
                    sp.dma_start(picks, picks_in).then_inc(s_epk, 16)
                if s == NG + 1:
                    sp.wait_ge(s_p, G * (NG - RING + 2))
                    sp.dma_start(wfs, Wf.rearrange("(c p) d -> p c d", p=P)).then_inc(s_ew, 16)

            def run(s, on):
                if on[5]:
                    stacked(s + 1)
                else:
                    epilogue_loads(s)
            steps(sp, run)

            for b in range(B):
                sp.wait_ge(s_fin, b + 1)
                sp.dma_start(out[b * T:b * T + T, :].rearrange("(n p) d -> p n d", p=P),
                             ey[b].rearrange("p (n d) -> p n d", n=QT)).then_inc(s_out, 16)
            sp.wait_ge(s_out, 16 * B)

        @block.gpsimd
        def _(pool):
            for i in range(2):
                pool.memset(cx[i][:, :, D:D + 1], 1.0)
            pool.memset(ones[:], 1.0)
            pool.memset(eps5[:], 1e-5)
            pool.memset(eps12[:], 1e-12)
            pool.memset(c_aim[:], float(NK - 2 * (TOPK - AIM)))
            pool.memset(c_one[:], 1.0)
            pool.memset(c_one4[:], 1.0)
            pool.memset(c_stiff[:], STIFF)
            pool.memset(c_neg[:], -1.0)
            pool.memset(ratio[:], 1.0)
            pool.drain().then_inc(s_cset1, 1)
            pool.memset(kst_flat[:], 0.0)
            pool.memset(qst[:], 0.0)
            pool.drain().then_inc(s_cset, 1)

            def correct(g, r, h):
                c = col(g * G + h * G // 2, G // 2)
                pool.wait_ge(s_cnt[r], G * g + (h + 1) * G // 2)
                pool.tensor_tensor(g_wait[:], c_one[:], c_one[:], ALU.mult)
                pool.tensor_tensor(g_f[:], c_aim[:], sgn[:, c], ALU.subtract)
                pool.drain()
                if r > 0:
                    pool.tensor_tensor(g_df[:], fprev[:, c], g_f[:], ALU.subtract)
                    pool.tensor_tensor(g_old[:], ratio[:, c], c_stiff[:], ALU.mult)
                    pool.drain()
                    pool.tensor_tensor(g_num[:], step_c[:, c], g_df[:], ALU.mult)
                    pool.tensor_tensor(g_den[:], g_df[:], g_df[:], ALU.mult)
                    pool.drain()
                    pool.tensor_tensor(g_num[:], g_num[:], g_old[:], ALU.add)
                    pool.tensor_tensor(g_den[:], g_den[:], c_stiff[:], ALU.add)
                    pool.drain()
                    pool.tensor_tensor(g_den[:], g_den[:], c_neg[:], ALU.pow)
                    pool.drain()
                    pool.tensor_tensor(g_r[:], g_num[:], g_den[:], ALU.mult)
                    pool.drain()
                    pool.tensor_scalar(g_r[:], g_r[:], 0.4, 2.2, ALU.max, ALU.min)
                    pool.drain()
                    pool.tensor_tensor(g_d[:], g_f[:], g_r[:], ALU.mult)
                else:
                    pool.tensor_tensor(g_d[:], g_f[:], c_one[:], ALU.mult)
                if r < 2:
                    pool.tensor_tensor(fprev[:, c], g_f[:], c_one[:], ALU.mult)
                    if r > 0:
                        pool.tensor_tensor(ratio[:, c], g_r[:], c_one[:], ALU.mult)
                    pool.drain()
                    pool.tensor_tensor(step_c[:, c], g_d[:], c_one[:], ALU.mult)
                else:
                    pool.drain()
                    pool.tensor_scalar(g_num[:], g_d[:], 0.0, 2 * LEAN, ALU.max, ALU.mult)
                    pool.tensor_scalar(g_den[:], g_d[:], 1 - LEAN, 2.0 * (LAST_AIM - AIM), ALU.mult, ALU.add)
                    pool.drain()
                    pool.tensor_tensor(g_d[:], g_num[:], g_den[:], ALU.add)
                    pool.drain()
                pool.tensor_tensor(g_e[:], g_d[:], unit[:, c], ALU.mult)
                pool.drain()
                pool.tensor_tensor(trial[:, c], trial[:, c], g_e[:], ALU.add).then_inc(s_thr[r + 1], 1)

            def settle(g):
                n = NV - 1
                pool.wait_ge(s_top, g + 1)
                pool.tensor_tensor(hit[:], ranks[:].unsqueeze(1).broadcast_to([P, G, n]),
                                   rank[:].unsqueeze(2).broadcast_to([P, G, n]), ALU.subtract)
                pool.tensor_tensor(bad2[:], top[:, :, 1], trial[:, col(g * G, G)], ALU.subtract)
                pool.drain()
                pool.tensor_scalar(hit[:], hit[:], 0.0, None, ALU.is_equal)
                pool.tensor_scalar(bad2[:], bad2[:], 0.0, None, ALU.is_lt)
                pool.drain()
                pool.tensor_tensor(pick[:, 0:G, :], hit[:], top[:, :, 0:n], ALU.mult)
                pool.tensor_tensor(pick[:, G:2 * G, :], hit[:], top[:, :, 1:n + 1], ALU.mult)
                pool.drain()
                while n > 3:
                    m = (n + 1) // 2
                    pool.tensor_tensor(pick[:, :, 0:n - m], pick[:, :, 0:n - m], pick[:, :, m:n], ALU.add)
                    pool.drain()
                    n = m
                pool.tensor_tensor(pick[:, :, 0], pick[:, :, 0], pick[:, :, 1], ALU.add)
                pool.drain()
                pool.tensor_tensor(sums[:], pick[:, :, 0], pick[:, :, 2], ALU.add)
                pool.drain()
                pool.tensor_tensor(bad[:], seg8[:], thr4, ALU.subtract)
                pool.tensor_scalar(found[:], thr4, 0.0, None, ALU.is_gt)
                pool.tensor_tensor(thr[:, col(g * G, G)], thr4, c_one4[:], ALU.mult)
                pool.tensor_tensor(nxt, nxt, thr4, ALU.subtract)
                pool.drain()
                pool.tensor_scalar(bad[:], bad[:], 0.0, None, ALU.is_lt)
                pool.tensor_scalar(nxt, nxt, 0.0, None, ALU.is_equal)
                pool.drain()
                pool.tensor_tensor(bad[:], bad[:], bad2[:], ALU.mult)
                pool.drain()
                pool.tensor_tensor(bad[:], bad[:], found[:], ALU.mult)
                pool.drain()
                pool.tensor_scalar(bad[:], bad[:], -LOST, LOST, ALU.mult, ALU.add)
                pool.drain()
                pool.tensor_tensor(bad[:], bad[:], nxt, ALU.add).then_inc(s_badr, 1)

            pool.wait_ge(s_st0, B)

            def run(s, on):
                if on[1]:
                    for h in range(2):
                        correct(s - 1, 0, h)
                if not on[0] and s == NG:
                    pool.wait_ge(s_ex, 16 * B)
                    for h in range(B):
                        pool.tensor_tensor(xb[h].rearrange("p (n d) -> p n d", n=QT),
                                           xb[h].rearrange("p (n d) -> p n d", n=QT),
                                           bob[:].unsqueeze(1).broadcast_to([P, QT, D]), ALU.add).then_inc(s_exb, 1)
                if on[1]:
                    for r in range(1, 3):
                        for h in range(2):
                            correct(s - 1, r, h)
                if on[2]:
                    settle(s - 2)
                if not on[0] and s == NG:
                    pool.wait_ge(s_epk, 16)
                    pool.tensor_copy(picks_b, picks).then_inc(s_epb, 1)
            steps(pool, run)

            pool.wait_ge(s_p, G * (NG - RING + 3))
            for h in range(B):
                pool.wait_ge(s_xn, h + 1)
                for dst, src, vec in ((xnb, xn2, bfb), (x1b, x1, beb)):
                    pool.tensor_tensor(dst[h].rearrange("p (n d) -> p n d", n=QT),
                                       src[h].rearrange("p (n d) -> p n d", n=QT),
                                       vec[:].unsqueeze(1).broadcast_to([P, QT, D]), ALU.add).then_inc(s_ads, 1)

        @block.scalar
        def _(act):
            act.wait_ge(s_cset1, 1)
            act.wait_ge(s_w, 16 * NW)
            for b in range(B + 1):
                if b < B:
                    act.wait_ge(s_pst, b + 1)
                    act.activation(rstd, agg[:, :, 1], ACT.Sqrt, bias=eps5[:]).then_inc(s_psd, 1)
                if b > 0:
                    act.wait_ge(s_kr, b)
                    act.activation(kp[(b - 1) % 2][1], kres, ACT.Copy).then_inc(s_k1, 1)
                if b < B:
                    act.wait_ge(s_k, b + 1)
                    if b >= 2:
                        act.wait_ge(s_pout[b % 2], 12 * 16)
                        act.wait_ge(s_kr, b - 1)
                    act.activation(kf[b % 2], psf[:, 0:NK], ACT.Identity, bias=bkc[:])
                    act.activation(kp[b % 2][0], psf[:, 0:NK], ACT.Identity, bias=bkc[:]).then_inc(s_kc, 1)
                if b > 0:
                    act.wait_ge(s_vmc, b)
                    act.activation(sig, var, ACT.Sqrt).then_inc(s_sg, 1)
                if b < B:
                    act.wait_ge(s_pxt, b + 1)
                    act.activation(xnT, ps[:, 6, 0:L], ACT.Copy).then_inc(s_pxc, 1)
            act.wait_ge(s_st0, B)

            def count(g, r, k):
                t = g * G + k
                if r == 0:
                    if k == 0 and (not isinstance(g, int) or g >= 1):
                        act.wait_ge(s_cnt[3], G * g)
                    act.wait_ge(s_ev, 2 * G * g + 2 * k + 2)
                elif k % 2 == 0:
                    act.wait_ge(s_thr[r], 2 * g + k // 2 + 1)
                    act.activation(a_wait[:, k // 2:k // 2 + 1], ones[:], ACT.Copy)
                act.activation(signs[:, k, :], S_at(g % RING, k), ACT.Sign, bias=trial[:, col(t)], scale=-1.0,
                               accum_out=sgn[:, col(t)]).then_inc(s_cnt[r], 1)

            def copy_transposed(g, k):
                act.wait_ge(s_t, g * G + k + 1)
                if k >= 2 or not isinstance(g, int) or g >= 1:
                    act.wait_ge(s_av, g * G + k - 1)
                for i in range(3):
                    act.activation(PT[k % 2][:, 4 * i:4 * i + 4, :],
                                   ps[:, 4 + i, :].rearrange("p (c q) -> p c q", c=4), ACT.Copy)
                act.activation(PT[k % 2][0:KR, 12, :], ps[0:KR, 7, 0:P], ACT.Copy).then_inc(s_cb, 1)

            def heads_back(h):
                act.wait_ge(s_hb, h + 1)
                act.activation(ecnT[h], ps_chain(h), ACT.Copy).then_inc(s_hc, 1)

            def deviation(h):
                act.wait_ge(s_st1, h + 1)
                act.activation(estd[h], eag[h][:, :, 1], ACT.Sqrt, bias=eps5[:]).then_inc(s_sd1, 1)

            def normed_T(h):
                act.wait_ge(s_xt, h + 1)
                act.activation(xnT2[h], ps_chain(h), ACT.Copy).then_inc(s_xc, 1)

            def choice_T(h):
                act.wait_ge(s_ot, h + 1)
                act.activation(oneT_b[h], ps_chain(h)[0:NE, :], ACT.Copy)
                act.activation(oneT[h], ps_chain(h)[0:NE, :], ACT.Copy).then_inc(s_oc, 1)

            def gelu(h):
                act.wait_ge(s_xu, NE * (h + 1))
                for c in range(NI // P):
                    act.activation(hT[h][:, c, :], ps_up(h, c), ACT.Gelu).then_inc(s_gl, 1)

            def last_deviation(h):
                act.wait_ge(s_st2, h + 1)
                act.activation(estd[h], eag[h][:, :, 1], ACT.Sqrt, bias=eps12[:]).then_inc(s_sd2, 1)

            def early_parts(s, k):
                for b in range(B - 1):
                    if (s, k) == (NG, 1):
                        heads_back(b)
                    if (s, k) == (NG, 2):
                        deviation(b)
                    if (s, k) == (NG, 3):
                        normed_T(b)
                    if (s, k) == (NG + 1, 0):
                        choice_T(b)
                if (s, k) == (NG + 3, 0):
                    gelu(0)

            def run(s, on):
                for k in range(G):
                    if on[1]:
                        count(s - 1, k, 0)
                        count(s - 1, k, 1)
                    if on[3]:
                        t = (s - 3) * G + k
                        if k == 0:
                            act.wait_ge(s_sel, s - 2)
                        if k >= 2 or not isinstance(s, int) or s > 3:
                            act.wait_ge(s_t, t - 1)
                        act.activation(E[k % 2][:], S_at((s - 3) % RING, k), ACT.Exp,
                                       bias=nmax[:, col(t)]).then_inc(s_exp, 1)
                    if k in (1, 2) and on[3]:
                        copy_transposed(s - 3, k - 1)
                    if on[1]:
                        count(s - 1, k, 2)
                        count(s - 1, k, 3)
                    if k == 0 and on[4]:
                        copy_transposed(s - 4, G - 1)
                    if k == 3 and on[3]:
                        copy_transposed(s - 3, 2)
                    if not on[0]:
                        early_parts(s, k)
            steps(act, run)

            heads_back(3)
            deviation(3)
            last_deviation(0)
            normed_T(3)
            choice_T(3)
            for b in range(1, B):
                gelu(b)
                last_deviation(b)

        @block.tensor
        def _(pe):
            pe.wait_ge(s_w, 16 * NW)

            def values(b, first, last, done):
                if first == 0:
                    pe.wait_ge(s_pin[b % 2], 64 * (b // 2 + 1))
                    if b > 0:
                        pe.wait_ge(s_vbc, b)
                else:
                    pe.wait_ge(s_vac, b + 1)
                for c in range(first, last):
                    m = P if c < KC - 1 else KR
                    mm = pe.matmul(ps[0:m, 4 + (c - first) // 4, (c - first) % 4 * D:(c - first) % 4 * D + D],
                                   cT[b % 2][:, c * P:c * P + m], wv, start=True, stop=True)
                mm.then_inc(done, 1)

            def keys(b, first):
                if b > 0:
                    pe.wait_ge(s_kc, b)
                for c in range(first, first + 2):
                    n = min(512, NK - 512 * c)
                    mm = pe.matmul(ps[:, c, 0:n], wk, cT[b % 2][:, 512 * c:512 * c + n], start=True, stop=True)
                if first == 2:
                    mm.then_inc(s_k, 1)

            def moments_by_k(b):
                pe.wait_ge(s_mc, b + 1)
                pe.matmul(ps[:, 7, 0:D], gram[:, 0:D], wk, start=True, stop=True)
                pe.matmul(ps[0:1, 7, D:2 * D], gram[:, D:D + 1], wk, start=True, stop=True)
                pe.matmul(ps[:, 7, 2 * D:2 * D + 1], wk, gram[:, D:D + 1], start=True, stop=True).then_inc(s_mk2, 1)

            def covariance(b):
                pe.wait_ge(s_mk2c, b + 1)
                pe.matmul(ps[:, 7, 0:D], wk, t1, start=True, stop=False)
                pe.matmul(ps[:, 7, 0:D], krow[0:1, :], nkrow[0:1, :], start=False, stop=True).then_inc(s_cv, 1)

            def spread(b):
                pe.wait_ge(s_cvc, b + 1)
                pe.wait_ge(s_qp, b + 1)
                pe.matmul(ps[:, 6, 0:L], cov, qf[b % 2], start=True, stop=True).then_inc(s_z, 1)

            def variance(b):
                pe.wait_ge(s_zc, b + 1)
                for t in range(QT):
                    q = slice(t * P, t * P + P)
                    pe.matmul(ps[:, 7, t * 32:t * 32 + H], zq[:, q], heads1[:], start=True, stop=True)
                    mm = pe.matmul(ps[:, 7, t * 32 + H:t * 32 + 2 * H], qf[b % 2][:, q], mb, start=True, stop=True)
                mm.then_inc(s_vm, 1)

            def queries(b):
                pe.wait_ge(s_pxn, b + 1)
                for t in range(QT):
                    mm = pe.transpose(ps[:, 6, t * P:t * P + P], xn[:, t, :], ident[:])
                mm.then_inc(s_pxt, 1)
                if b == 0:
                    pe.wait_ge(s_cset1, 1)
                else:
                    pe.wait_ge(s_vmc, b)
                for c in range(KC):
                    m = P if c < KC - 1 else KR
                    mm = pe.matmul(ps[:, 7, 0:D + 1], cx[b % 2][0:m, c, 0:D], cx[b % 2][0:m, c, :],
                                   start=(c == 0), stop=(c == KC - 1))
                mm.then_inc(s_m, 1)
                pe.wait_ge(s_pxc, b + 1)
                pe.matmul(ps[:, 6, 0:L], wq, xnT, start=True, stop=True).then_inc(s_q, 1)

            for b in range(B + 1):
                if b < B:
                    values(b, 0, 8, s_va)
                if b > 0:
                    moments_by_k(b - 1)
                if b < B:
                    keys(b, 0)
                if b > 0:
                    covariance(b - 1)
                if b < B:
                    keys(b, 2)
                if b > 0:
                    spread(b - 1)
                if b < B:
                    values(b, 8, KC, s_vb)
                if b > 0:
                    variance(b - 1)
                if b < B:
                    queries(b)
            pe.wait_ge(s_st0, B)

            def transposes(g, k):
                t = g * G + k
                pe.wait_ge(s_p, t + 1)
                if not isinstance(g, int) or t >= 1:
                    pe.wait_ge(s_cb, t)
                for c in range(KC):
                    m = P if c < KC - 1 else KR
                    mm = pe.transpose(ps[0:m, 4 + c // 4, c % 4 * P:c % 4 * P + P],
                                      E[k % 2][:, c * P:c * P + m], ident[:])
                mm.then_inc(s_t, 1)

            def head(g, k):
                t = g * G + k
                pe.wait_ge(s_cb, t + 1)
                if k == 0 and (not isinstance(g, int) or g >= 1):
                    pe.wait_ge(s_ao, g)
                for c in range(KC):
                    m = P if c < KC - 1 else KR
                    mm = pe.matmul(ps_heads[:, k * DH:k * DH + DH], PT[k % 2][0:m, c, :],
                                   V_all[0:m, c, bass.ds(g * 2 * DH + k // QT * DH, DH)],
                                   start=(c == 0), stop=(c == KC - 1))
                mm.then_inc(s_av, 1)

            def marks(g):
                pe.wait_ge(s_badr, g + 1)
                pe.matmul(ps_bad, ones[:], bad[:], start=True, stop=True).then_inc(s_badc, 1)

            def scores(s, k):
                if k == 0:
                    pe.wait_ge(s_stk, 96 * (s + 1))
                slot = s % 2 * 2 + k // 2
                for piece in range(2):
                    if not isinstance(s, int) or s * G + k >= 1:
                        pe.wait_ge(s_ev, 2 * G * s + 2 * k - 1 + piece)
                    a, e = (0, CUT) if piece == 0 else (CUT, NK)
                    while a < e:
                        n = min(512, e - a)
                        mm = pe.matmul(psf[:, a:a + n], qst[:, bass.ds(slot, 1), k % 2 * P:k % 2 * P + P]
                                       .rearrange("p a q -> p (a q)"),
                                       kst[:, bass.ds(slot, 1), a:a + n].rearrange("p a k -> p (a k)"),
                                       start=True, stop=True)
                        a += n
                    mm.then_inc(s_sc, 1)

            def heads_back(h):
                pe.wait_ge(s_hn, h + 1)
                if h == 3:
                    pe.wait_ge(s_cb, NT)
                for t in range(QT):
                    mm = pe.transpose(ps_chain(h)[:, t * P:t * P + P], ecn[h][:, t * P:t * P + P], ident[:])
                mm.then_inc(s_hb, 1)

            def project(h):
                pe.wait_ge(s_hc, h + 1)
                for t in range(QT):
                    mm = pe.matmul(ps_chain(h)[:, t * P:t * P + P], ecnT[h][:, t * P:t * P + P], wo[:],
                                   start=True, stop=True)
                mm.then_inc(s_wo, 1)

            def normed_T(h):
                pe.wait_ge(s_xn, h + 1)
                for t in range(QT):
                    mm = pe.transpose(ps_chain(h)[:, t * P:t * P + P], xn2[h][:, t * P:t * P + P], ident[:])
                mm.then_inc(s_xt, 1)

            def route(h):
                pe.wait_ge(s_xc, h + 1)
                for t in range(QT):
                    mm = pe.matmul(ps_chain(h)[:, t * NE:t * NE + NE], xnT2[h][:, t * P:t * P + P], wr[:],
                                   start=True, stop=True)
                mm.then_inc(s_rt, 1)

            def choice_T(h):
                pe.wait_ge(s_one, h + 1)
                for t in range(QT):
                    mm = pe.transpose(ps_chain(h)[0:NE, t * P:t * P + P], eone[h][:, t, :], ident[:])
                mm.then_inc(s_ot, 1)

            def mask(h, e):
                if h + e == 0:
                    pe.wait_ge(s_epb, 1)
                if e == 0:
                    pe.wait_ge(s_oc, max(h + 1, 3))
                if h + e > 0:
                    pe.wait_ge(s_xm, h * NE + e)
                pe.matmul(ps_mask, picks_b[:, e * P:e * P + P], oneT_b[h], start=True, stop=True).then_inc(s_mk, 1)

            def up(h, e):
                if e == 0:
                    mask(h, 0)
                    pe.wait_ge(s_ew, 96)
                    if h == 1:
                        pe.wait_ge(s_gl, NI // P)
                    if h == 2:
                        pe.wait_ge(s_cb, NT)
                    if h == 3:
                        pe.wait_ge(s_gl, 2 * NI // P)
                    for c in range(NI // P):
                        pe.matmul(ps_up(h, c), b1s[0:NE, c * P:c * P + P], oneT[h],
                                  start=(c % 2 == 0), stop=False)
                pe.wait_ge(s_xm, h * NE + e + 1)
                if e + 1 < NE:
                    mask(h, e + 1)
                for c in range(NI // P):
                    mm = pe.matmul(ps_up(h, c), w1_at(e, c), xm[e % 2][:, 0:T],
                                   start=False, stop=(e == NE - 1 and c % 2 == 1))
                mm.then_inc(s_xu, 1)

            def down(h):
                pe.wait_ge(s_gl, NI // P * (h + 1))
                if h == 0:
                    pe.wait_ge(s_cb, NT)
                else:
                    pe.wait_ge(s_st2, h)
                for t in range(QT):
                    for c in range(NI // P):
                        mm = pe.matmul(ps_down[:, t * P:t * P + P], hT[h][:, c, t * P:t * P + P], wfs[:, c, :],
                                       start=(c == 0), stop=(c == NI // P - 1))
                mm.then_inc(s_dn, 1)

            def early_parts(s, k):
                for b in range(B - 1):
                    if (s, k) == (NG, 0):
                        heads_back(b)
                    if (s, k) == (NG, 1):
                        project(b)
                    if (s, k) == (NG, 2):
                        normed_T(b)
                    if (s, k) == (NG, 3):
                        route(b)
                if (s, k) == (NG + 1, 0):
                    for b in range(B - 1):
                        choice_T(b)
                if s == NG + 1 and k > 0:
                    up(0, k - 1)
                if s == NG + 2:
                    up(0, 3 + k)
                if (s, k) == (NG + 3, 0):
                    up(0, 7)

            scores(0, 0)

            def run(s, on):
                for k in range(G):
                    if on[0] and k < G - 1:
                        scores(s, k + 1)
                    if on[5] and k == G - 1:
                        scores(s + 1, 0)
                    if k == 2 and on[0] and not on[5]:
                        pe.wait_ge(s_ev, 2 * NT - 2)
                    if k == 0 and not on[0] and on[3]:
                        pe.wait_ge(s_bad, s - 2)
                    if k < 2 and on[4]:
                        head(s - 4, k + 2)
                    if k == 2 and on[3]:
                        head(s - 3, 0)
                        head(s - 3, 1)
                    if k == 3 and on[2]:
                        if on[0] and not on[5]:
                            pe.wait_ge(s_ev, 2 * NT)
                        marks(s - 2)
                    if on[3]:
                        transposes(s - 3, k)
                    if not on[0]:
                        early_parts(s, k)
            steps(pe, run)

            down(0)
            up(1, 0)
            heads_back(3)
            up(1, 1)
            project(3)
            up(1, 2)
            up(1, 3)
            normed_T(3)
            up(1, 4)
            route(3)
            up(1, 5)
            choice_T(3)
            up(1, 6)
            up(1, 7)
            for b in range(2, B):
                for e in range(NE):
                    up(b, e)
                    if e == 1:
                        down(b - 1)
            down(3)

        @block.vector
        def _(dve):
            dve.wait_ge(s_cset1, 1)

            def x_statistics(b):
                dve.wait_ge(s_pin[b % 2], 64 * (b // 2 + 1))
                for t in range(QT):
                    dve.bn_stats(stats[:, t, :], xin[b % 2][:, t, :])
                dve.drain()
                for t in range(QT):
                    ins = dve.bn_aggr(agg[:, t, :], stats[:, t, :])
                ins.then_inc(s_pst, 1)

            def norm_x(b):
                dve.wait_ge(s_psd, b + 1)
                dve.reciprocal(rstd, rstd)
                dve.drain()
                for t in range(QT):
                    ins = dve.tensor_scalar(xn[:, t, :], xin[b % 2][:, t, :], agg[:, t, 0:1], rstd[:, t:t + 1],
                                            ALU.subtract, ALU.mult)
                ins.then_inc(s_pxn, 1)

            def copy_values(b, first, last, ready, done):
                n = min(last, KC - 1) - first
                vps = psf[:, 4 * 512:4 * 512 + 8 * D].rearrange("p (c d) -> p c d", c=8)
                dve.wait_ge(ready, b + 1)
                ins = dve.tensor_tensor(V_all[:, first:first + n, b * D:b * D + D], vps[:, 0:n, :],
                                        bvb.unsqueeze(1).broadcast_to([P, n, D]), ALU.add)
                if last == KC:
                    ins = dve.tensor_tensor(V_all[0:KR, KC - 1, b * D:b * D + D], vps[0:KR, n, :],
                                            bvb[0:KR, :], ALU.add)
                ins.then_inc(done, 1)

            def copy_moments_by_k(b):
                dve.wait_ge(s_mk2, b + 1)
                dve.tensor_copy(t1, ps[:, 7, 0:D])
                dve.tensor_copy(krow[0:1, :], ps[0:1, 7, D:2 * D])
                dve.tensor_scalar(nkrow[0:1, :], ps[0:1, 7, D:2 * D], -1.0, None, ALU.mult)
                dve.tensor_tensor(kb, ps[:, 7, 2 * D:2 * D + 1], bkc[:], ALU.add)
                dve.drain()
                dve.tensor_scalar(mb, heads1[:], kb, None, ALU.mult).then_inc(s_mk2c, 1)

            def mask_covariance(b):
                dve.wait_ge(s_cv, b + 1)
                dve.tensor_tensor(cov, ps[:, 7, 0:D], blocks, ALU.mult).then_inc(s_cvc, 1)

            def copy_spread(b):
                dve.wait_ge(s_z, b + 1)
                dve.tensor_tensor(zq, ps[:, 6, 0:L], qf[b % 2], ALU.mult).then_inc(s_zc, 1)

            def copy_variance(b):
                dve.wait_ge(s_vm, b + 1)
                st = ps[:, 7, 0:QT * 32].rearrange("p (t s) -> p t s", t=QT)
                dve.tensor_copy(mean, st[:, :, H:2 * H])
                dve.tensor_scalar(var, st[:, :, 0:H], 0.0, None, ALU.max).then_inc(s_vmc, 1)

            def search_starts(b):
                dve.wait_ge(s_sg, b + 1)
                c = bass.ds(b * H * QT, H * QT)
                by_t = lambda arr: arr[:, c].rearrange("p (h t) -> p t h", t=QT)
                dve.tensor_scalar(by_t(unit), sig, SLOPE, None, ALU.mult)
                dve.tensor_scalar(by_t(trial), sig, SHIFT, None, ALU.mult)
                dve.scalar_tensor_tensor(by_t(shift), sig, SHIFT, mean, ALU.mult, ALU.subtract).then_inc(s_st0, 1)

            def key_residual(b, i):
                if i == 0:
                    dve.wait_ge(s_kc, b + 1)
                    dve.tensor_tensor(kres, kf[b % 2], kp[b % 2][0], ALU.subtract).then_inc(s_kr, 1)
                else:
                    dve.wait_ge(s_k1, b + 1)
                    dve.tensor_tensor(kp[b % 2][2], kres, kp[b % 2][1], ALU.subtract).then_inc(s_kp, 1)

            def query_parts(b):
                dve.wait_ge(s_m, b + 1)
                dve.tensor_scalar(gram, ps[:, 7, 0:D + 1], 1.0 / NK, None, ALU.mult).then_inc(s_mc, 1)
                dve.wait_ge(s_q, b + 1)
                if b >= 2:
                    dve.wait_ge(s_pout[b % 2], 12 * 16)
                q, (q0, q1, q2) = qf[b % 2], qp[b % 2]
                dve.tensor_scalar(q, ps[:, 6, 0:L], bqc[:], QSCALE, ALU.add, ALU.mult)
                dve.drain()
                dve.tensor_copy(q0, q)
                dve.drain()
                dve.tensor_tensor(qres, q, q0, ALU.subtract)
                dve.drain()
                dve.tensor_copy(q1, qres)
                dve.drain()
                dve.tensor_tensor(q2, qres, q1, ALU.subtract).then_inc(s_qp, 1)

            for b in range(B + 1):
                if b < B:
                    x_statistics(b)
                if b > 0:
                    key_residual(b - 1, 0)
                    copy_moments_by_k(b - 1)
                if b == 0:
                    dve.wait_ge(s_w, 16 * NW)
                    dve.wait_ge(s_const, 16 * NCONST)
                if b < B:
                    copy_values(b, 0, 8, s_va, s_vac)
                if b > 0:
                    mask_covariance(b - 1)
                if b < B:
                    norm_x(b)
                if b > 0:
                    key_residual(b - 1, 1)
                    copy_spread(b - 1)
                if b < B:
                    copy_values(b, 8, KC, s_vb, s_vbc)
                if b > 0:
                    copy_variance(b - 1)
                if b < B:
                    query_parts(b)
                if b > 0:
                    search_starts(b - 1)

            for i in range(2):
                dve.wait_ge(s_pout[i], 12 * 16 * (B // 2))

            def select(g, k):
                t = g * G + k
                dve.wait_ge(s_cnt[3], t + 1)
                sc = S_at(g % RING, k)
                dve.scalar_tensor_tensor(y[k % 2][:], sc, trial[:, col(t)], sc, ALU.is_le, ALU.mult)
                dve.drain()

            def candidates(k):
                for i in range(NSEG):
                    e = (i + 1) * SEG if i < NSEG - 1 else NK
                    dve.max(cand[:, k, 8 * i:8 * i + 8], y[k % 2][:, i * SEG:e])

            def order(g):
                dve.drain()
                for i in range(3):
                    src = cand if i == 0 else cand2
                    for k in range(G):
                        dve.max(top[:, k, 8 * i:8 * i + 8], src[:, k, :])
                    if i == 0:
                        dve.tensor_scalar(rank[:], sgn[:, col(g * G, G)], 0.5, TOPK - NK / 2 + 0.25, ALU.mult, ALU.add)
                        dve.tensor_reduce(seg8[:], cand[:, :, 7:8 * NSEG:8], AX.X, ALU.max)
                    if i < 2:
                        dve.drain()
                        for k in range(G):
                            dve.match_replace(cand2[:, k, :], top[:, k, 8 * i:8 * i + 8], src[:, k, :], 0.0)
                        if i == 0:
                            dve.tensor_scalar(rank[:], rank[:], 2.0 ** 23, -2.0 ** 23, ALU.add, ALU.add)
                        dve.drain()
                dve.drain().then_inc(s_top, 1)

            def bisect(g, k):
                t = g * G + k
                sc = S_at(g % RING, k)
                top_s = nmax[:, col(t)]
                dve.tensor_scalar(y[0][:], sc, 1.0, None, ALU.mult, ALU.min, accum_out=lo[:])
                dve.tensor_scalar(mid[:], top_s, -1.0, None, ALU.mult)
                dve.drain()
                dve.tensor_tensor(hi[:], mid[:], lo[:], ALU.subtract)
                dve.tensor_tensor(w0[:], mid[:], top_s, ALU.max)
                dve.drain()
                dve.tensor_tensor(hi[:], hi[:], mid[:], ALU.add)
                dve.drain()
                dve.scalar_tensor_tensor(hi[:], hi[:], 1.0 / BIG, w0[:], ALU.add, ALU.add)
                dve.drain()
                with dve.Fori(0, BISECT):
                    dve.tensor_tensor(mid[:], lo[:], hi[:], ALU.add)
                    dve.drain()
                    dve.tensor_scalar(mid[:], mid[:], 0.5, None, ALU.mult)
                    dve.drain()
                    dve.tensor_scalar(y[0][:], sc, mid[:], None, ALU.is_ge, ALU.add, accum_out=cnt[:])
                    dve.drain()
                    dve.tensor_scalar(keep[:], cnt[:], TOPK - 0.5, None, ALU.is_ge)
                    dve.drain()
                    dve.tensor_scalar(w0[:], keep[:], 1.0, BIG, ALU.subtract, ALU.mult)
                    dve.tensor_tensor(w1[:], keep[:], mid[:], ALU.mult)
                    dve.drain()
                    dve.tensor_tensor(w0[:], w0[:], w1[:], ALU.add)
                    dve.tensor_tensor(w2[:], mid[:], w1[:], ALU.subtract)
                    dve.drain()
                    dve.tensor_tensor(lo[:], lo[:], w0[:], ALU.max)
                    dve.scalar_tensor_tensor(w2[:], keep[:], BIG, w2[:], ALU.mult, ALU.add)
                    dve.drain()
                    dve.tensor_tensor(hi[:], hi[:], w2[:], ALU.min)
                    dve.drain()

            def break_tie(g, k, above, under):
                t = g * G + k
                sc = S_at(g % RING, k)
                dve.tensor_scalar(y[0][:], sc, hi[:], None, above, ALU.add, accum_out=cnt[:])
                dve.drain()
                dve.tensor_scalar(keep[:], cnt[:], -1.0, float(TOPK), ALU.mult, ALU.add)
                dve.tensor_scalar(y[0][:], sc, lo[:], 0.5, ALU.is_ge, ALU.mult)
                dve.drain()
                dve.scalar_tensor_tensor(y[0][:], sc, hi[:], y[0][:], under, ALU.mult)
                dve.drain()
                dve.tensor_tensor_scan(y[0][:], y[0][:], y[0][:], 0.0, ALU.add, ALU.add)
                dve.drain()
                dve.tensor_scalar(y[0][:], y[0][:], keep[:], -BIG, ALU.is_gt, ALU.mult)
                dve.drain()
                dve.scalar_tensor_tensor(y[0][:], sc, hi[:], y[0][:], under, ALU.mult)
                dve.drain()
                dve.tensor_tensor(sc, sc, y[0][:], ALU.add)
                dve.tensor_copy(thr[:, col(t)], lo[:])
                dve.drain()

            def heads_out(g):
                dve.wait_ge(s_av, G * (g + 1))
                dve.tensor_copy(heads_q[:, bass.ds(g * G * DH, G * DH)], ps_heads).then_inc(s_ao, 1)

            def by_tile(a):
                return a.rearrange("p (n d) -> p n d", d=D)

            def divide(h):
                a = h * H * QT
                dve.reciprocal(rz[h].rearrange("p (t a) -> p t a", t=QT),
                               Z[:, a:a + H * QT].rearrange("p (a t) -> p t a", t=QT))
                dve.drain()
                dve.wait_ge(s_ao, NG // B * (h + 1))
                hq = heads_q[:, h * H * QT * DH:(h + 1) * H * QT * DH].rearrange("p (a t d) -> p t a d", t=QT, d=DH)
                for t in range(QT):
                    ins = dve.tensor_tensor(ecn[h][:, t * P:t * P + P].rearrange("p (a d) -> p a d", d=DH),
                                            hq[:, t, :, :],
                                            rz[h][:, t * H:t * H + H].unsqueeze(2).broadcast_to([P, H, DH]), ALU.mult)
                ins.then_inc(s_hn, 1)

            def statistics(src, h):
                for t in range(QT):
                    dve.bn_stats(est[h][:, t, :], src[h][:, t * P:t * P + P])
                dve.drain()
                for t in range(QT):
                    ins = dve.bn_aggr(eag[h][:, t, :], est[h][:, t, :])
                return ins

            def residual(h):
                dve.wait_ge(s_exb, h + 1)
                dve.wait_ge(s_wo, h + 1)
                dve.tensor_tensor(x1[h], ps_chain(h), xb[h], ALU.add)
                dve.drain()
                statistics(x1, h).then_inc(s_st1, 1)

            def norm(h):
                dve.wait_ge(s_sd1, h + 1)
                dve.reciprocal(estd[h], estd[h])
                dve.drain()
                for t in range(QT):
                    q = slice(t * P, t * P + P)
                    ins = dve.tensor_scalar(xn2[h][:, q], x1[h][:, q], eag[h][:, t, 0:1], estd[h][:, t:t + 1],
                                            ALU.subtract, ALU.mult)
                ins.then_inc(s_xn, 1)

            def choose(h):
                logits = ps_chain(h)[:, 0:QT * NE].rearrange("p (t e) -> p t e", e=NE)
                top1 = emx[h].unsqueeze(2).broadcast_to([P, QT, NE])
                dve.wait_ge(s_rt, h + 1)
                dve.tensor_reduce(emx[h], logits, AX.X, ALU.max)
                dve.drain()
                dve.tensor_tensor(elog[h], logits, top1, ALU.is_equal)
                dve.drain()
                dve.tensor_tensor(elog[h], elog[h], firsts[:].unsqueeze(1).broadcast_to([P, QT, NE]), ALU.mult)
                dve.drain()
                dve.tensor_reduce(emx[h], elog[h], AX.X, ALU.max)
                dve.drain()
                dve.tensor_tensor(eone[h], elog[h], top1, ALU.is_equal).then_inc(s_one, 1)

            def tokens(h, e):
                if h * NE + e >= 2:
                    dve.wait_ge(s_xu, h * NE + e - 1)
                dve.wait_ge(s_mk, h * NE + e + 1)
                dve.wait_ge(s_xc, h + 1)
                dve.tensor_tensor(xm[e % 2][:, 0:T], ps_mask, xnT2[h], ALU.mult).then_inc(s_xm, 1)

            def add_up(h):
                dve.wait_ge(s_ads, 2 * h + 2)
                dve.wait_ge(s_dn, h + 1)
                dve.tensor_tensor(ey[h], ps_down, xnb[h], ALU.add)
                dve.drain()
                statistics(ey, h).then_inc(s_st2, 1)

            def finish(h):
                dve.wait_ge(s_sd2, h + 1)
                dve.reciprocal(estd[h], estd[h])
                dve.drain()
                for t in range(QT):
                    q = slice(t * P, t * P + P)
                    dve.tensor_scalar(ey[h][:, q], ey[h][:, q], eag[h][:, t, 0:1], estd[h][:, t:t + 1],
                                      ALU.subtract, ALU.mult)
                dve.drain()
                dve.tensor_tensor(by_tile(ey[h]), by_tile(ey[h]), gab[:].unsqueeze(1).broadcast_to([P, QT, D]), ALU.mult)
                dve.drain()
                dve.tensor_tensor(ey[h], ey[h], x1b[h], ALU.add).then_inc(s_fin, 1)

            def early_parts(s, k):
                for b in range(B - 1):
                    if (s, k) == (NG, 0):
                        divide(b)
                    if (s, k) == (NG, 1):
                        residual(b)
                    if (s, k) == (NG, 2):
                        norm(b)
                    if (s, k) == (NG + 1, 0):
                        choose(b)
                if s == NG + 1 and k > 0:
                    tokens(0, k - 1)
                if s == NG + 2:
                    tokens(0, 3 + k)
                if (s, k) == (NG + 3, 0):
                    tokens(0, 7)

            def run(s, on):
                for k in range(G):
                    if on[0]:
                        t = s * G + k
                        for piece in range(2):
                            a, n = (0, CUT) if piece == 0 else (CUT, NK - CUT)
                            dve.wait_ge(s_sc, 2 * t + piece + 1)
                            if piece == 1 and (on[4] or on[3] and k == 3):
                                dve.wait_ge(s_av, (s - 3) * G + (2 if k == 3 else k - 2))
                            if piece == 1 and k == 2 and on[4]:
                                heads_out(s - 4)
                            dve.tensor_scalar(S_at(s % RING, k, a, n), psf[:, a:a + n], shift[:, col(t)], None,
                                              ALU.add, ALU.max, accum_out=mx[:, k, piece:piece + 1]
                                              ).then_inc(s_ev, 1)
                    if k == 2 and on[4] and not on[0]:
                        heads_out(s - 4)
                    if on[2]:
                        if k == 0:
                            select(s - 2, 0)
                        if k == 1:
                            candidates(1)
                        if k == 2:
                            select(s - 2, 3)
                            candidates(3)
                            order(s - 2)
                    if on[3]:
                        g = s - 3
                        dve.wait_ge(s_exp, g * G + k + 1)
                        e = E[k % 2][:]
                        dve.scalar_tensor_tensor(e, S_at(g % RING, k), thr[:, col(g * G + k)], e,
                                                 ALU.is_ge, ALU.mult,
                                                 accum_out=Z[:, col(g * G + k)]).then_inc(s_p, 1)
                    if on[2]:
                        if k == 0:
                            candidates(0)
                            select(s - 2, 1)
                        if k == 1:
                            select(s - 2, 2)
                            candidates(2)
                    if not on[0]:
                        early_parts(s, k)
                if on[0]:
                    dve.drain()
                    dve.tensor_tensor(nmax[:, col(s * G, G)], mx[:, :, 0], mx[:, :, 1], ALU.max)
                    dve.drain()
                    dve.tensor_scalar(nmax[:, col(s * G, G)], nmax[:, col(s * G, G)], -1.0, None, ALU.mult)
                if on[2]:
                    g = s - 2
                    dve.wait_ge(s_badc, g + 1)
                    dve.tensor_copy(badi[:, 0:G], ps_bad)
                    dve.tensor_reduce(badf[:], ps_bad, AX.X, ALU.add).then_inc(s_bad, 1)
                    dve.drain()
                    dve.tensor_copy(badi[:, G:G + 1], badf[:])
                    dve.drain()
                    rows = dve.value_load(badi[0:1, G:G + 1], min_val=0, max_val=G * MOST)
                    with dve.If(rows > 0):
                        with dve.Fori(0, G) as k:
                            mine = dve.value_load(badi[0:1, bass.ds(k, 1)], min_val=0, max_val=MOST)
                            with dve.If(mine >= int(LOST)):
                                bisect(g, k)
                                break_tie(g, k, ALU.is_ge, ALU.is_lt)
                            with dve.Else():
                                with dve.If(mine > 0):
                                    dve.tensor_copy(lo[:], thr[:, col(g * G + k)])
                                    dve.tensor_copy(hi[:], thr[:, col(g * G + k)])
                                    dve.drain()
                                    break_tie(g, k, ALU.is_gt, ALU.is_le)
                    dve.drain().then_inc(s_sel, 1)
            steps(dve, run)

            tokens(1, 0)
            divide(3)
            add_up(0)
            tokens(1, 1)
            tokens(1, 2)
            residual(3)
            tokens(1, 3)
            norm(3)
            tokens(1, 4)
            tokens(1, 5)
            choose(3)
            tokens(1, 6)
            finish(0)
            tokens(1, 7)
            for b in range(2, B):
                for e in range(NE):
                    tokens(b, e)
                    if e == 2:
                        add_up(b - 1)
                    if e == 4:
                        finish(b - 1)
            add_up(3)
            finish(3)


def kernel(**inputs):
    import concourse.bacc as bacc
    from concourse.bass_utils import run_bass_kernel_spmd as run

    nc = bacc.Bacc("TRN2", target_bir_lowering=False, num_devices=1)
    a = {k: np.asarray(v) for k, v in inputs.items()}
    head_of = np.arange(P) // DH
    arrays = {
        "x": a["x"].reshape(B * L, D),
        "ctx": a["ctx_1024"].reshape(B * NK, D),
        "ctxT": a["ctx_1024"].transpose(0, 2, 1).reshape(B * D, NK),
        "WqT": a["L0_xattn_Wq"].T, "bq": a["L0_xattn_bq"],
        "WkT": a["L0_xattn_Wk"].T, "bk": a["L0_xattn_bk"],
        "WvT": a["L0_xattn_Wv"].T, "bv": a["L0_xattn_bv"],
        "WoT": a["L0_xattn_Wo"].T, "bo": a["L0_xattn_bo"],
        "WrT": a["L0_ffn_Wr"].T, "W1": a["L0_ffn_W1"], "b1": a["L0_ffn_b1"],
        "Wf": a["L0_ffn_Wo"], "bf": a["L0_ffn_bo"],
        "gamma": a["L0_ffn_gamma"], "beta": a["L0_ffn_beta"],
        "ident": np.eye(P, dtype=np.float32),
        "blocks": (head_of[:, None] == head_of[None, :]).astype(np.float32),
        "heads": (head_of[:, None] == np.arange(H)[None, :]).astype(np.float32),
        "ranks": np.tile(np.arange(1, NV, dtype=np.float32), (P, 1)),
        "firsts": np.tile(np.arange(NE, 0, -1, dtype=np.float32), (P, 1)),
        "picks": np.repeat(np.eye(NE, dtype=np.float32), P, axis=1),
    }
    args = []
    for name in arrays:
        arrays[name] = np.ascontiguousarray(arrays[name])
        args.append(nc.dram_tensor(f"in_{name}", arrays[name].shape, F32, kind="ExternalInput").ap())
    args.append(nc.dram_tensor("out", (B * L, D), F32, kind="ExternalOutput").ap())
    build(nc, *args)
    r = run(nc, [{f"in_{k}": v for k, v in arrays.items()}], core_ids=[0])
    return r.results[0]["out"].reshape(B, L, D)
```
